# Optimizing a Trainium2 kernel written in Bass

```python
import numpy as np
import jax
import jax.numpy as jnp

def _softmax(x, axis=-1):
    return jax.nn.softmax(x, axis=axis)

def _gelu(x):
    return jax.nn.gelu(x, approximate=True)

def _silu(x):
    return jax.nn.silu(x)

def _sigmoid(x):
    return jax.nn.sigmoid(x)

def _layernorm(x, axis=-1, eps=1e-05):
    m = jnp.mean(x, axis=axis, keepdims=True)
    v = jnp.var(x, axis=axis, keepdims=True)
    return (x - m) / jnp.sqrt(v + eps)

def _scatter_add(tgt, idx, src, axis=0):
    return tgt.at[idx].add(src)

def _segment_sum(src, seg, n):
    return jax.ops.segment_sum(src, seg, n)
kernel_name = 'mk_gnn_preln_d4_gnn_r8_c0774e'

def setup_inputs(seed: int=0):
    np.random.seed(seed)
    _w = jnp.asarray

    def _rec_inputs():
        import jax
        import jax.numpy as jnp
        _gk = jax.random.key(seed)
        x = -0.000202 + 1 * jax.random.normal(jax.random.fold_in(_gk, 1), (6250, 128), jnp.float32)
        src = jax.random.randint(jax.random.fold_in(_gk, 2), (100000,), 0, 6250, jnp.int32)
        dst = jax.random.randint(jax.random.fold_in(_gk, 3), (100000,), 0, 6250, jnp.int32)
        _o = jnp.argsort(dst, stable=True)
        src = src[_o]
        dst = dst[_o]
        edge_attr_64 = 0.000167468 + 1.0002 * jax.random.normal(jax.random.fold_in(_gk, 12), (100000, 64), jnp.float32)
        edge_weight1 = jax.random.uniform(jax.random.fold_in(_gk, 14), (100000, 1), jnp.float32, 0.0, 0.999998)
        return (x, src, dst, edge_attr_64, edge_weight1)
    x, src, dst, edge_attr_64, edge_weight1 = _rec_inputs()

    def _L0_gnn_setup():
        import jax, jax.numpy as jnp
        import numpy as np
        N_NODES = 6250
        N_EDGES = 100000
        DIM = 128
        key = jax.random.key(seed)
        k1, k2, k3, k4, k5, k6 = jax.random.split(key, 6)
        x = jax.random.normal(k1, (N_NODES, DIM), dtype=jnp.float32)
        edge_index = jax.random.randint(k2, (2, N_EDGES), 0, N_NODES, dtype=jnp.int64)
        W_w = jax.random.normal(k3, (DIM, DIM), dtype=jnp.float32) * (1.0 / np.sqrt(DIM))
        W_b = jax.random.normal(k4, (DIM,), dtype=jnp.float32) * 0.01
        a_w = jax.random.normal(k5, (2 * DIM, 1), dtype=jnp.float32) * (1.0 / np.sqrt(2 * DIM))
        a_b = jax.random.normal(k6, (1,), dtype=jnp.float32) * 0.01
        return {'x': x, 'edge_index': edge_index, 'W_w': W_w, 'W_b': W_b, 'a_w': a_w, 'a_b': a_b}
    _L0_gnn_all = _L0_gnn_setup()
    _L0_gnn_in = {k: v for k, v in _L0_gnn_all.items() if k in ('W_w', 'W_b', 'a_w', 'a_b')}
    del _L0_gnn_all

    def _L1_gnn_setup():
        import jax, jax.numpy as jnp
        import numpy as np
        N_NODES = 5000
        N_EDGES = 80000
        N_GRAPHS = 64
        NODE_NF = 128
        EDGE_NF = 64
        GLOBAL_NF = 64
        HIDDEN_NF = 128
        key = jax.random.key(seed)
        ks = jax.random.split(key, 16)
        x = jax.random.normal(ks[0], (N_NODES, NODE_NF), dtype=jnp.float32)
        edge_index = jax.random.randint(ks[1], (2, N_EDGES), 0, N_NODES, dtype=jnp.int64)
        edge_attr = jax.random.normal(ks[2], (N_EDGES, EDGE_NF), dtype=jnp.float32)
        u = jax.random.normal(ks[3], (N_GRAPHS, GLOBAL_NF), dtype=jnp.float32)
        batch = jnp.sort(jax.random.randint(ks[4], (N_NODES,), 0, N_GRAPHS, dtype=jnp.int64))

        def lin(k, fin, fout):
            s = 1.0 / np.sqrt(fin)
            kw, kb = jax.random.split(k)
            W = jax.random.uniform(kw, (fin, fout), minval=-s, maxval=s, dtype=jnp.float32)
            b = jax.random.uniform(kb, (fout,), minval=-s, maxval=s, dtype=jnp.float32)
            return (W, b)
        W1a, b1a = lin(ks[5], NODE_NF + EDGE_NF, HIDDEN_NF)
        W1b, b1b = lin(ks[6], HIDDEN_NF, HIDDEN_NF)
        W2a, b2a = lin(ks[7], NODE_NF + HIDDEN_NF + GLOBAL_NF, HIDDEN_NF)
        W2b, b2b = lin(ks[8], HIDDEN_NF, NODE_NF)
        return {'x': x, 'edge_index': edge_index, 'edge_attr': edge_attr, 'u': u, 'batch': batch, 'W1a': W1a, 'b1a': b1a, 'W1b': W1b, 'b1b': b1b, 'W2a': W2a, 'b2a': b2a, 'W2b': W2b, 'b2b': b2b}
    _L1_gnn_all = _L1_gnn_setup()
    _L1_gnn_in = {k: v for k, v in _L1_gnn_all.items() if k in ('u', 'W1a', 'b1a', 'W1b', 'b1b', 'W2a', 'b2a', 'W2b', 'b2b')}
    del _L1_gnn_all

    def _L2_gnn_setup():
        import jax, jax.numpy as jnp
        import numpy as np
        N, E, IN, HID, H, OUT = (6250, 100000, 128, 64, 4, 128)
        NEG = 0.2
        EPS = 1e-05

        def _seg_softmax(a, seg, n):
            amax = jax.lax.stop_gradient(jax.ops.segment_max(a, seg, num_segments=n))
            amax = jnp.where(jnp.isfinite(amax), amax, 0.0)
            ex = jnp.exp(a - amax[seg])
            den = jax.ops.segment_sum(ex, seg, num_segments=n)
            return ex / (den[seg] + 1e-16)

        def _gatv2(x, src, dst, e_attr, Wl, bl, Wr, br, We, att, bias, heads, c, concat):
            n = x.shape[0]
            xl = (x @ Wl + bl).reshape(n, heads, c)
            xr = (x @ Wr + br).reshape(n, heads, c)
            ee = (e_attr @ We).reshape(-1, heads, c)
            m = xl[src] + xr[dst] + ee
            m = jnp.where(m > 0, m, NEG * m)
            alpha = _seg_softmax(jnp.einsum('ehc,hc->eh', m, att), dst, n)
            out = jax.ops.segment_sum(alpha[:, :, None] * xl[src], dst, num_segments=n)
            out = out.reshape(n, heads * c) if concat else out.mean(axis=1)
            return out + bias

        def _bn(h, g, b):
            mu = jnp.mean(h, axis=0)
            var = jnp.var(h, axis=0)
            return (h - mu) * jax.lax.rsqrt(var + EPS) * g + b

        def _prelu(h, a):
            return jnp.where(h > 0, h, a * h)
        key = jax.random.key(seed)
        ks = jax.random.split(key, 16)

        def nrm(k, shape, fan):
            return jax.random.normal(k, shape, jnp.float32) / np.float32(np.sqrt(fan))
        x = jax.random.normal(ks[0], (N, IN), jnp.float32)
        edge_index = jax.random.randint(ks[1], (2, E), 0, N, jnp.int32)
        edge_attr = jax.random.uniform(ks[2], (E, 1), dtype=jnp.float32)
        return {'x': x, 'edge_index': edge_index, 'edge_attr': edge_attr, 'Wl1': nrm(ks[3], (IN, H * HID), IN), 'bl1': jnp.zeros((H * HID,), jnp.float32), 'Wr1': nrm(ks[4], (IN, H * HID), IN), 'br1': jnp.zeros((H * HID,), jnp.float32), 'We1': nrm(ks[5], (1, H * HID), 1), 'att1': nrm(ks[6], (H, HID), HID), 'cb1': jnp.zeros((H * HID,), jnp.float32), 'bng1': jnp.ones((H * HID,), jnp.float32), 'bnb1': jnp.zeros((H * HID,), jnp.float32), 'pa': jnp.float32(0.25), 'Wl2': nrm(ks[7], (H * HID, OUT), H * HID), 'bl2': jnp.zeros((OUT,), jnp.float32), 'Wr2': nrm(ks[8], (H * HID, OUT), H * HID), 'br2': jnp.zeros((OUT,), jnp.float32), 'We2': nrm(ks[9], (1, OUT), 1), 'att2': nrm(ks[10], (1, OUT), OUT), 'cb2': jnp.zeros((OUT,), jnp.float32), 'bng2': jnp.ones((OUT,), jnp.float32), 'bnb2': jnp.zeros((OUT,), jnp.float32), 'skipW': nrm(ks[11], (IN, OUT), IN), 'skipb': jnp.zeros((OUT,), jnp.float32)}
    _L2_gnn_all = _L2_gnn_setup()
    _L2_gnn_in = {k: v for k, v in _L2_gnn_all.items() if k in ('Wl1', 'bl1', 'Wr1', 'br1', 'We1', 'att1', 'cb1', 'bng1', 'bnb1', 'pa', 'Wl2', 'bl2', 'Wr2', 'br2', 'We2', 'att2', 'cb2', 'bng2', 'bnb2', 'skipW', 'skipb')}
    del _L2_gnn_all

    def _L3_gnn_setup():
        import jax, jax.numpy as jnp
        import numpy as np
        N_NODES = 6250
        N_EDGES = 100000
        C_IN = 128
        HID = 128
        C_OUT = 128

        def _glorot(key, shape):
            fan_in, fan_out = shape
            lim = (6.0 / (fan_in + fan_out)) ** 0.5
            return jax.random.uniform(key, shape, jnp.float32, -lim, lim)

        def _edge_conv(x, src, dst, W1, b1, W2, b2, n_nodes):
            xi = x[dst]
            xj = x[src]
            m = jnp.concatenate([xi, xj - xi], axis=-1)
            h = jax.nn.relu(m @ W1 + b1) @ W2 + b2
            agg = jax.ops.segment_max(h, dst, num_segments=n_nodes)
            return jnp.where(jnp.isfinite(agg), agg, 0.0)
        key = jax.random.key(seed)
        ks = jax.random.split(key, 8)
        x = jax.random.normal(ks[0], (N_NODES, C_IN), jnp.float32)
        edge_index = jax.random.randint(ks[1], (2, N_EDGES), 0, N_NODES, jnp.int32)
        return {'x': x, 'edge_index': edge_index, 'W1_in': _glorot(ks[2], (2 * C_IN, HID)), 'b1_in': jnp.zeros((HID,), jnp.float32), 'W2_in': _glorot(ks[3], (HID, HID)), 'b2_in': jnp.zeros((HID,), jnp.float32), 'W1_hid': _glorot(ks[4], (2 * HID, HID)), 'b1_hid': jnp.zeros((HID,), jnp.float32), 'W2_hid': _glorot(ks[5], (HID, HID)), 'b2_hid': jnp.zeros((HID,), jnp.float32), 'W1_out': _glorot(ks[6], (2 * HID, HID)), 'b1_out': jnp.zeros((HID,), jnp.float32), 'W2_out': _glorot(ks[7], (HID, C_OUT)), 'b2_out': jnp.zeros((C_OUT,), jnp.float32)}
    _L3_gnn_all = _L3_gnn_setup()
    _L3_gnn_in = {k: v for k, v in _L3_gnn_all.items() if k in ('W1_in', 'b1_in', 'W2_in', 'b2_in', 'W1_hid', 'b1_hid', 'W2_hid', 'b2_hid', 'W1_out', 'b1_out', 'W2_out', 'b2_out')}
    del _L3_gnn_all
    return {'x': x, 'src': src, 'dst': dst, 'edge_attr_64': edge_attr_64, 'edge_weight1': edge_weight1, 'L0_gnn_W_w': _L0_gnn_in['W_w'], 'L0_gnn_W_b': _L0_gnn_in['W_b'], 'L0_gnn_a_w': _L0_gnn_in['a_w'], 'L0_gnn_a_b': _L0_gnn_in['a_b'], 'L1_gnn_u': _L1_gnn_in['u'], 'L1_gnn_W1a': _L1_gnn_in['W1a'], 'L1_gnn_b1a': _L1_gnn_in['b1a'], 'L1_gnn_W1b': _L1_gnn_in['W1b'], 'L1_gnn_b1b': _L1_gnn_in['b1b'], 'L1_gnn_W2a': _L1_gnn_in['W2a'], 'L1_gnn_b2a': _L1_gnn_in['b2a'], 'L1_gnn_W2b': _L1_gnn_in['W2b'], 'L1_gnn_b2b': _L1_gnn_in['b2b'], 'L2_gnn_Wl1': _L2_gnn_in['Wl1'], 'L2_gnn_bl1': _L2_gnn_in['bl1'], 'L2_gnn_Wr1': _L2_gnn_in['Wr1'], 'L2_gnn_br1': _L2_gnn_in['br1'], 'L2_gnn_We1': _L2_gnn_in['We1'], 'L2_gnn_att1': _L2_gnn_in['att1'], 'L2_gnn_cb1': _L2_gnn_in['cb1'], 'L2_gnn_bng1': _L2_gnn_in['bng1'], 'L2_gnn_bnb1': _L2_gnn_in['bnb1'], 'L2_gnn_pa': _L2_gnn_in['pa'], 'L2_gnn_Wl2': _L2_gnn_in['Wl2'], 'L2_gnn_bl2': _L2_gnn_in['bl2'], 'L2_gnn_Wr2': _L2_gnn_in['Wr2'], 'L2_gnn_br2': _L2_gnn_in['br2'], 'L2_gnn_We2': _L2_gnn_in['We2'], 'L2_gnn_att2': _L2_gnn_in['att2'], 'L2_gnn_cb2': _L2_gnn_in['cb2'], 'L2_gnn_bng2': _L2_gnn_in['bng2'], 'L2_gnn_bnb2': _L2_gnn_in['bnb2'], 'L2_gnn_skipW': _L2_gnn_in['skipW'], 'L2_gnn_skipb': _L2_gnn_in['skipb'], 'L3_gnn_W1_in': _L3_gnn_in['W1_in'], 'L3_gnn_b1_in': _L3_gnn_in['b1_in'], 'L3_gnn_W2_in': _L3_gnn_in['W2_in'], 'L3_gnn_b2_in': _L3_gnn_in['b2_in'], 'L3_gnn_W1_hid': _L3_gnn_in['W1_hid'], 'L3_gnn_b1_hid': _L3_gnn_in['b1_hid'], 'L3_gnn_W2_hid': _L3_gnn_in['W2_hid'], 'L3_gnn_b2_hid': _L3_gnn_in['b2_hid'], 'L3_gnn_W1_out': _L3_gnn_in['W1_out'], 'L3_gnn_b1_out': _L3_gnn_in['b1_out'], 'L3_gnn_W2_out': _L3_gnn_in['W2_out'], 'L3_gnn_b2_out': _L3_gnn_in['b2_out']}

def reference(x, src, dst, edge_attr_64, edge_weight1, L0_gnn_W_w, L0_gnn_W_b, L0_gnn_a_w, L0_gnn_a_b, L1_gnn_u, L1_gnn_W1a, L1_gnn_b1a, L1_gnn_W1b, L1_gnn_b1b, L1_gnn_W2a, L1_gnn_b2a, L1_gnn_W2b, L1_gnn_b2b, L2_gnn_Wl1, L2_gnn_bl1, L2_gnn_Wr1, L2_gnn_br1, L2_gnn_We1, L2_gnn_att1, L2_gnn_cb1, L2_gnn_bng1, L2_gnn_bnb1, L2_gnn_pa, L2_gnn_Wl2, L2_gnn_bl2, L2_gnn_Wr2, L2_gnn_br2, L2_gnn_We2, L2_gnn_att2, L2_gnn_cb2, L2_gnn_bng2, L2_gnn_bnb2, L2_gnn_skipW, L2_gnn_skipb, L3_gnn_W1_in, L3_gnn_b1_in, L3_gnn_W2_in, L3_gnn_b2_in, L3_gnn_W1_hid, L3_gnn_b1_hid, L3_gnn_W2_hid, L3_gnn_b2_hid, L3_gnn_W1_out, L3_gnn_b1_out, L3_gnn_W2_out, L3_gnn_b2_out):
    import jax
    import jax.numpy as jnp

    def _L0_gnn_ref(x, edge_index, W_w, W_b, a_w, a_b):
        import jax, jax.numpy as jnp
        import numpy as np
        N_NODES = 6250
        N_EDGES = 100000
        DIM = 128
        h = x @ W_w + W_b
        row, col = (edge_index[0], edge_index[1])
        a_src, a_dst = (a_w[:DIM], a_w[DIM:])
        e = h[row] @ a_src + h[col] @ a_dst + a_b
        e = jax.nn.leaky_relu(e, negative_slope=0.01)
        attention = jax.nn.softmax(e, axis=0)
        msg = attention * h[col]
        out = jax.ops.segment_sum(msg, row, num_segments=N_NODES)
        return out

    def _L1_gnn_ref(x, edge_index, edge_attr, u, batch, W1a, b1a, W1b, b1b, W2a, b2a, W2b, b2b):
        import jax, jax.numpy as jnp
        import numpy as np
        N_NODES = 5000
        N_EDGES = 80000
        N_GRAPHS = 64
        NODE_NF = 128
        EDGE_NF = 64
        GLOBAL_NF = 64
        HIDDEN_NF = 128
        row, col = (edge_index[0], edge_index[1])
        n_nodes = x.shape[0]
        h = jnp.concatenate([x[row], edge_attr], axis=1)
        h = jax.nn.relu(h @ W1a + b1a) @ W1b + b1b
        sums = jax.ops.segment_sum(h, col, num_segments=n_nodes)
        counts = jax.ops.segment_sum(jnp.ones((h.shape[0],), dtype=h.dtype), col, num_segments=n_nodes)
        agg = sums / jnp.clip(counts, 1.0)[:, None]
        z = jnp.concatenate([x, agg, u[batch]], axis=1)
        return jax.nn.relu(z @ W2a + b2a) @ W2b + b2b

    def _L2_gnn_ref(x, edge_index, edge_attr, Wl1, bl1, Wr1, br1, We1, att1, cb1, bng1, bnb1, pa, Wl2, bl2, Wr2, br2, We2, att2, cb2, bng2, bnb2, skipW, skipb):
        import jax, jax.numpy as jnp
        import numpy as np
        N, E, IN, HID, H, OUT = (6250, 100000, 128, 64, 4, 128)
        NEG = 0.2
        EPS = 1e-05

        def _seg_softmax(a, seg, n):
            amax = jax.lax.stop_gradient(jax.ops.segment_max(a, seg, num_segments=n))
            amax = jnp.where(jnp.isfinite(amax), amax, 0.0)
            ex = jnp.exp(a - amax[seg])
            den = jax.ops.segment_sum(ex, seg, num_segments=n)
            return ex / (den[seg] + 1e-16)

        def _gatv2(x, src, dst, e_attr, Wl, bl, Wr, br, We, att, bias, heads, c, concat):
            n = x.shape[0]
            xl = (x @ Wl + bl).reshape(n, heads, c)
            xr = (x @ Wr + br).reshape(n, heads, c)
            ee = (e_attr @ We).reshape(-1, heads, c)
            m = xl[src] + xr[dst] + ee
            m = jnp.where(m > 0, m, NEG * m)
            alpha = _seg_softmax(jnp.einsum('ehc,hc->eh', m, att), dst, n)
            out = jax.ops.segment_sum(alpha[:, :, None] * xl[src], dst, num_segments=n)
            out = out.reshape(n, heads * c) if concat else out.mean(axis=1)
            return out + bias

        def _bn(h, g, b):
            mu = jnp.mean(h, axis=0)
            var = jnp.var(h, axis=0)
            return (h - mu) * jax.lax.rsqrt(var + EPS) * g + b

        def _prelu(h, a):
            return jnp.where(h > 0, h, a * h)
        src, dst = (edge_index[0], edge_index[1])
        h = _gatv2(x, src, dst, edge_attr, Wl1, bl1, Wr1, br1, We1, att1, cb1, H, HID, True)
        h = _prelu(_bn(h, bng1, bnb1), pa)
        h = _gatv2(h, src, dst, edge_attr, Wl2, bl2, Wr2, br2, We2, att2, cb2, 1, OUT, False)
        h = _prelu(_bn(h, bng2, bnb2), pa)
        return h + (x @ skipW + skipb)

    def _L3_gnn_ref(x, edge_index, W1_in, b1_in, W2_in, b2_in, W1_hid, b1_hid, W2_hid, b2_hid, W1_out, b1_out, W2_out, b2_out):
        import jax, jax.numpy as jnp
        import numpy as np
        N_NODES = 6250
        N_EDGES = 100000
        C_IN = 128
        HID = 128
        C_OUT = 128

        def _glorot(key, shape):
            fan_in, fan_out = shape
            lim = (6.0 / (fan_in + fan_out)) ** 0.5
            return jax.random.uniform(key, shape, jnp.float32, -lim, lim)

        def _edge_conv(x, src, dst, W1, b1, W2, b2, n_nodes):
            xi = x[dst]
            xj = x[src]
            m = jnp.concatenate([xi, xj - xi], axis=-1)
            h = jax.nn.relu(m @ W1 + b1) @ W2 + b2
            agg = jax.ops.segment_max(h, dst, num_segments=n_nodes)
            return jnp.where(jnp.isfinite(agg), agg, 0.0)
        src, dst = (edge_index[0], edge_index[1])
        n = x.shape[0]
        x = _edge_conv(x, src, dst, W1_in, b1_in, W2_in, b2_in, n)
        x = jax.nn.relu(x)
        x = _edge_conv(x, src, dst, W1_hid, b1_hid, W2_hid, b2_hid, n)
        x = jax.nn.relu(x)
        x = _edge_conv(x, src, dst, W1_out, b1_out, W2_out, b2_out, n)
        return x
    edge_index = jnp.stack([src, dst])
    batch0 = jnp.zeros((6250,), jnp.int32)
    h = jnp.maximum(_layernorm(x, axis=-1), 0.0)
    x = x + _L0_gnn_ref(h, edge_index, L0_gnn_W_w, L0_gnn_W_b, L0_gnn_a_w, L0_gnn_a_b)
    h = jnp.maximum(_layernorm(x, axis=-1), 0.0)
    x = x + _L1_gnn_ref(h, edge_index, edge_attr_64, L1_gnn_u, batch0, L1_gnn_W1a, L1_gnn_b1a, L1_gnn_W1b, L1_gnn_b1b, L1_gnn_W2a, L1_gnn_b2a, L1_gnn_W2b, L1_gnn_b2b)
    h = jnp.maximum(_layernorm(x, axis=-1), 0.0)
    x = x + _L2_gnn_ref(h, edge_index, edge_weight1, L2_gnn_Wl1, L2_gnn_bl1, L2_gnn_Wr1, L2_gnn_br1, L2_gnn_We1, L2_gnn_att1, L2_gnn_cb1, L2_gnn_bng1, L2_gnn_bnb1, L2_gnn_pa, L2_gnn_Wl2, L2_gnn_bl2, L2_gnn_Wr2, L2_gnn_br2, L2_gnn_We2, L2_gnn_att2, L2_gnn_cb2, L2_gnn_bng2, L2_gnn_bnb2, L2_gnn_skipW, L2_gnn_skipb)
    h = jnp.maximum(_layernorm(x, axis=-1), 0.0)
    x = x + _L3_gnn_ref(h, edge_index, L3_gnn_W1_in, L3_gnn_b1_in, L3_gnn_W2_in, L3_gnn_b2_in, L3_gnn_W1_hid, L3_gnn_b1_hid, L3_gnn_W2_hid, L3_gnn_b2_hid, L3_gnn_W1_out, L3_gnn_b1_out, L3_gnn_W2_out, L3_gnn_b2_out)
    return x

_drawn_inputs = setup_inputs


def setup_inputs(seed=0):
    import zlib

    import numpy as np

    out = dict(_drawn_inputs(seed))
    spreads = {'L2_gnn_bl1': (0.0, 0.497),
     'L2_gnn_br1': (0.0, 0.463),
     'L2_gnn_cb1': (0.0, 2.0),
     'L2_gnn_bng1': (1.0, 0.2),
     'L2_gnn_bnb1': (0.0, 0.341),
     'L2_gnn_bl2': (0.0, 0.56),
     'L2_gnn_br2': (0.0, 0.482),
     'L2_gnn_cb2': (0.0, 2.0),
     'L2_gnn_bng2': (1.0, 0.2),
     'L2_gnn_bnb2': (0.0, 0.1),
     'L2_gnn_skipb': (0.0, 0.1),
     'L3_gnn_b1_in': (0.0, 0.298),
     'L3_gnn_b2_in': (0.0, 0.379),
     'L3_gnn_b1_hid': (0.0, 0.306),
     'L3_gnn_b2_hid': (0.0, 0.35),
     'L3_gnn_b1_out': (0.0, 0.28),
     'L3_gnn_b2_out': (0.0, 0.1)}
    factors = {'edge_attr_64': 8.0,
     'L0_gnn_W_w': 8.0,
     'L0_gnn_W_b': 64.0,
     'L0_gnn_a_w': 8.0,
     'L1_gnn_W1a': 5.293,
     'L1_gnn_b1a': 8.0,
     'L1_gnn_W1b': 3.299,
     'L1_gnn_b1b': 7.212,
     'L1_gnn_b2a': 3.978}
    for name, (base, spread) in spreads.items():
        noise = np.random.default_rng([zlib.crc32(name.encode()), seed]).standard_normal(out[name].shape)
        drawn = base * np.exp(spread * noise) if base else spread * noise
        out[name] = jnp.asarray(drawn.astype(out[name].dtype))
    for name, factor in factors.items():
        out[name] = (out[name] * factor).astype(out[name].dtype)
    return out
```

```python
from contextlib import ExitStack

import numpy as np

import concourse.bass as bass
from concourse import mybir

FP32, I32 = mybir.dt.float32, mybir.dt.int32
ALU, ACT, AX = mybir.AluOpType, mybir.ActivationFunctionType, mybir.AxisListType

P = 128
NODES, EDGES, DIM, EDGE_DIM = 6250, 100000, 128, 64
BLOCKS = -(-NODES // P)
ROWS = BLOCKS * P
TILES = -(-EDGES // P)
GROUP, TURN = 4, 8
STEPS = -(-(TILES + BLOCKS - 1) // TURN) * TURN
TURNS = STEPS // TURN
CHUNKS = -(-STEPS // P)
ALL = CHUNKS * P
NB = 7
HEADS, HID = 4, 64
WIDE = HEADS * HID
FAR = float(1 << 20)
BIG = 1.0e30
COPIES = 8
TRASH = ROWS


class Signal:

    def __init__(self, handle):
        self.h, self.base = handle, 0

    def at(self, n):
        return n + self.base

    def start(self, eng):
        eng.sem_inc(self.h, 1)

    def turn(self, j):
        return j + (self.base + 2)

    def last(self, j):
        return j + (self.base + 1)

    def passed(self, n):
        self.base += n


class Chain:

    def __init__(self, signal):
        self.s, self.k, self.j, self.per, self.eng = signal, 0, None, 0, None

    def on(self, eng):
        self.eng = eng
        return self

    def open(self, j, per):
        self.s.passed(self.k)
        self.k, self.j, self.per = 0, j, per

    def close(self, trips):
        assert self.k == self.per, (self.k, self.per)
        self.s.passed(self.per * trips)
        self.k, self.j = 0, None

    def link(self, ins):
        ins.then_inc(self.s.h, 1)
        self.k += 1
        n = self.s.at(self.k)
        self.eng.wait_ge(self.s.h, n if self.j is None else self.j * self.per + n)


def every(ap, n):
    return ap.unsqueeze(1).to_broadcast([ap.shape[0], n, ap.shape[1]])


def each(ap, n):
    return ap.unsqueeze(2).to_broadcast([ap.shape[0], ap.shape[1], n])


def build(nc, I, out, stop=9):
    ctx = ExitStack()
    with ctx:
        sb = lambda name, shape, dt=FP32: ctx.enter_context(nc.sbuf_tensor(name, shape, dt))
        sig = lambda name: Signal(ctx.enter_context(nc.semaphore(name)))
        dram = lambda name, shape: nc.dram_tensor(name, shape, FP32).ap()

        X = sb("X", [P, BLOCKS * DIM])
        H = sb("H", [P, BLOCKS * DIM])
        T1 = sb("T1", [P, BLOCKS * (WIDE + HEADS)])
        T2 = sb("T2", [P, BLOCKS * WIDE])
        W = sb("W", [P, 10 * DIM])
        iota = sb("iota", [P, P])
        ident = sb("ident", [P, P])
        ones = sb("ones", [P, P])
        lower = sb("lower", [P, P])
        pcol = sb("pcol", [P, 1])
        dloc = sb("dloc", [P, ALL])
        dend = sb("dend", [P, ALL])
        ew = sb("ew", [P, ALL])
        srci = sb("srci", [P, ALL], I32)
        brow = sb("brow", [1, ALL], I32)
        trow = sb("trow", [1, ALL], I32)
        LG = sb("LG", [P, HEADS * ALL])
        srcf = LG[:, 3 * ALL:4 * ALL]
        sidx = LG[:, 2 * ALL:2 * ALL + STEPS].bitcast(I32)
        cnt = sb("cnt", [P, BLOCKS])
        slot_idx = sb("slot_idx", [P, TURN], I32)
        goes_on = sb("goes_on", [HEADS, ALL])
        came_on = sb("came_on", [HEADS, ALL])
        pa_col = sb("pa_col", [P, 1])
        has = sb("has", [P, BLOCKS])
        small = sb("small", [P, 64])
        PS = ctx.enter_context(nc.psum_tensor("PS", [P, 4096], FP32))
        bank = lambda n, w=512: PS[:, 512 * n:512 * n + w]

        onehot_t_d = dram("onehot_t_d", [P, STEPS * P])
        packed_d = dram("packed_d", [ALL, 6 * P])
        step_src_d = dram("step_src_d", [ALL, P])
        step_dst_d = dram("step_dst_d", [ALL + 2, P])
        step_first_d = dram("step_first_d", [ALL, P])
        step_last_d = dram("step_last_d", [ALL, P])
        score_d = dram("score_d", [ROWS, 1])
        gather_d = dram("gather_d", [ROWS, DIM])
        wide_d = dram("wide_d", [ROWS, WIDE])
        edge_rows_d = dram("edge_rows_d", [P, STEPS * WIDE])
        ends_d = dram("ends_d", [HEADS, ALL + 2])
        ends2_d = dram("ends2_d", [HEADS, ALL + 2])
        added_d = [dram(f"added_{k}_d", [ROWS + P, DIM]) for k in range(COPIES)]

        vch, ach, gch = Chain(sig("vector_done")), Chain(sig("scalar_done")), Chain(sig("gpsimd_done"))
        loaded, stored = sig("loaded"), sig("stored")
        pe_done, ev_done, vv_done = sig("products_done"), sig("evicted"), sig("vector_ready")
        pe2_done, ac_done, v2_done = sig("products2_done"), sig("scalar_ready"), sig("vector2_ready")
        two = lambda name: [sig(f"{name}_{g}") for g in range(2)]
        rows_here, rows_free = two("rows_here"), two("rows_free")
        tiles_here, tiles_free = two("tiles_here"), two("tiles_free")
        extra_here, extra_free = two("extra_here"), two("extra_free")
        saved = two("saved")
        pool_gate = sig("pool_gate")
        pA, pB, pC, pD, pE = (two(f"product_{k}") for k in "abcde")
        vA, vB, vC, vD, vE = (two(f"vector_{k}") for k in "abcde")
        aA, aB, aC = (two(f"scalar_{k}") for k in "abc")
        one_hots = two("one_hots")
        scattered = [sig(f"scattered_{k}") for k in range(COPIES)]
        scattered_read = [sig(f"scattered_read_{k}") for k in range(COPIES)]
        gch_done = sig("reduced")
        V, S_, T_, G = nc.vector, nc.scalar, nc.tensor, nc.gpsimd

        def blocks(tab, width):
            return tab[:, 0:BLOCKS * width].rearrange("p (t w) -> p t w", w=width)

        def blocks_of(eng, j):
            return [eng.value_load(brow[0:1, bass.ds(j * TURN + u, 1)], min_val=0, max_val=BLOCKS - 1) for u in range(TURN)]

        def setup():
            raw = T2[:, 0:4 * CHUNKS * P].bitcast(I32).rearrange("p (k c e) -> p k c e", k=4, e=P)
            pk = T1[:, 0:6 * ALL].rearrange("p (c k e) -> p c k e", k=6, e=P)
            cmp = H[:, 0:CHUNKS * ALL].rearrange("p (c s) -> p c s", c=CHUNKS)
            far = LG[:, 0:ALL].rearrange("p (c e) -> p c e", e=P)
            ewr = LG[:, ALL:2 * ALL].rearrange("p (c e) -> p c e", e=P)
            iota_s = LG[:, 2 * ALL:3 * ALL]
            trep = LG[:, 3 * ALL:4 * ALL]
            stepr = T2[:, 4 * ALL:10 * ALL].rearrange("p (c k e) -> p c k e", k=6, e=P)
            key, tcol, bcol = small[:, 0:7], small[:, 8:15], small[:, 16:23]
            keyi, tcoli = small[:, 24:31].bitcast(I32), small[:, 32:39].bitcast(I32)
            scol = small[:, 40:47]
            cview = lambda flat, off: flat[off:off + ALL * P].rearrange("(c p e) -> p c e", p=P, e=P)
            with nc.Block() as block:
                @block.sync
                def _(sp):
                    for k, off in ((1, 1), (2, 0), (3, 2)):
                        sp.dma_start(raw[:, k], cview(I["dst"], off)).then_inc(loaded.h, 16)
                    sp.dma_start(raw[:, 0], cview(I["src"], 0)).then_inc(loaded.h, 16)
                    sp.dma_start(ewr, cview(I["ew"], 0)).then_inc(loaded.h, 16)
                    sp.dma_start(blocks(X, DIM), I["x"].rearrange("(t p) f -> p t f", p=P)).then_inc(loaded.h, 16)
                    sp.wait_ge(vv_done.h, 2)
                    sp.dma_start(packed_d.rearrange("(c p) w -> p c w", p=P),
                                 pk.rearrange("p c k e -> p c (k e)")).then_inc(stored.h, 16)
                    sp.wait_ge(vv_done.h, 5)
                    mid = step_dst_d[1:ALL + 1, :]
                    for k, d in ((0, step_src_d), (1, mid), (3, step_first_d), (4, step_last_d)):
                        sp.dma_start(d.rearrange("(c p) e -> p c e", p=P), stepr[:, :, k, :]).then_inc(stored.h, 16)
                    sp.dma_start(step_dst_d[0:1, :], W[0:1, 0:P]).then_inc(stored.h, 16)
                    sp.dma_start(step_dst_d[ALL + 1:ALL + 2, :], W[0:1, 0:P]).then_inc(stored.h, 16)
                    sp.wait_ge(stored.h, 16 * 7)
                    sp.wait_ge(loaded.h, 16 * 6)

                @block.gpsimd
                def _(gp):
                    c = gch.on(gp)
                    gp.iota(iota[:, :], pattern=[[1, P]], base=0, channel_multiplier=0, allow_small_or_imprecise_dtypes=True)
                    gp.iota(iota_s, pattern=[[1, ALL]], base=0, channel_multiplier=0, allow_small_or_imprecise_dtypes=True)
                    gp.iota(pcol[:, :], pattern=[[1, 1]], base=0, channel_multiplier=1, allow_small_or_imprecise_dtypes=True)
                    gp.iota(scol, pattern=[[P, CHUNKS]], base=0, channel_multiplier=1, allow_small_or_imprecise_dtypes=True)
                    gp.memset(W[0:1, 0:P], -FAR)
                    gp.memset(ones[:, :], 1.0)
                    gp.memset(lower[:, :], 1.0)
                    c.link(gp.memset(ident[:, :], 0.0))
                    gp.affine_select(out=lower[:, :], in_=lower[:, :], compare_op=ALU.is_gt, fill=0.0,
                                     base=0, pattern=[[-1, P]], channel_multiplier=1)
                    gp.affine_select(out=ident[:, :], in_=ident[:, :], compare_op=ALU.not_equal, fill=1.0,
                                     base=0, pattern=[[-1, P]], channel_multiplier=1).then_inc(ac_done.h, 1)
                    gp.wait_ge(vv_done.h, 4)
                    gp.sem_inc(pool_gate.h, 1)
                    gp.wait_ge(stored.h, 16)
                    for k in range(CHUNKS):
                        gp.indirect_dma_start(stepr[:, k].rearrange("p k e -> p (k e)"), None, packed_d[:, :],
                                              bass.IndirectOffsetOnAxis(ap=tcoli[:, k:k + 1], axis=0)).then_inc(rows_here[0].h, 16)

                @block.vector
                def _(dve):
                    c = vch.on(dve)
                    dve.wait_ge(loaded.h, 16 * 6)
                    dve.wait_ge(ac_done.h, 1)
                    V.tensor_copy(pk[:, :, 0], raw[:, 0])
                    V.tensor_copy(pk[:, :, 5], ewr)
                    V.tensor_single_scalar(keyi, raw[:, 1, :, 0], 7, ALU.arith_shift_right)
                    V.tensor_tensor(pk[:, :, 3], raw[:, 1], raw[:, 2], ALU.not_equal)
                    V.tensor_tensor(pk[:, :, 4], raw[:, 1], raw[:, 3], ALU.not_equal)
                    V.tensor_copy(pk[:, :, 1], raw[:, 1])
                    c.link(V.tensor_scalar(far, raw[:, 1], FAR, None, ALU.add))
                    V.tensor_tensor(key, keyi, scol, ALU.add)
                    c.link(V.tensor_tensor(far, far, pk[:, :, 4], ALU.mult))
                    V.tensor_scalar(pk[:, :, 2], far, -FAR, None, ALU.add)
                    V.tensor_scalar(pk[:, :, 3], pk[:, :, 3], -BIG, None, ALU.mult)
                    V.tensor_scalar(pk[:, :, 4], pk[:, :, 4], -BIG, None, ALU.mult).then_inc(vv_done.h, 2)
                    for k in range(CHUNKS):
                        last = V.tensor_scalar(cmp[:, k], iota_s, key[:, k:k + 1], None, ALU.is_ge)
                    last.then_inc(vv_done.h, 1)
                    dve.wait_ge(pe_done.h, 1)
                    half = ALL // 2
                    for h in range(2):
                        last = V.tensor_scalar(trep[:, h * half:(h + 1) * half], bank(h, half), -1.0, 0.0, ALU.add, ALU.max)
                    last.then_inc(v2_done.h, 1)
                    dve.wait_ge(v2_done.h, 1)
                    V.tensor_copy(trow[:, :], trep[0:1, :])
                    c.link(V.tensor_tensor(ewr.rearrange("p c e -> p (c e)"), iota_s, trep, ALU.subtract))
                    V.tensor_scalar(brow[:, :], LG[0:1, ALL:2 * ALL], float(BLOCKS - 1), None, ALU.min)
                    dve.wait_ge(pe_done.h, 2)
                    tr = PS[:, 1024:1024 + CHUNKS * P].rearrange("p (c e) -> p c e", e=P)[:, :, 0]
                    c.link(V.tensor_copy(tcol, tr))
                    V.tensor_copy(tcoli, tcol).then_inc(vv_done.h, 1)
                    c.link(V.tensor_tensor(bcol, scol, tcol, ALU.subtract))
                    c.link(V.tensor_scalar(bcol, bcol, float(P), None, ALU.mult))
                    dve.wait_ge(rows_here[0].h, 16 * CHUNKS)
                    for k in range(CHUNKS):
                        V.tensor_scalar(far[:, k], stepr[:, k, 1], bcol[:, k:k + 1], None, ALU.subtract)
                        last = V.tensor_scalar(stepr[:, k, 2], stepr[:, k, 2], bcol[:, k:k + 1], None, ALU.subtract)
                    last.then_inc(vv_done.h, 1)
                    for n, dst in enumerate((dloc, dend, ew, srci)):
                        dve.wait_ge(pe2_done.h, n + 1)
                        if n == 3:
                            V.tensor_copy(srcf[:, :], PS[:, 1024 * (n % 2):1024 * (n % 2) + ALL])
                        V.tensor_copy(dst[:, :], PS[:, 1024 * (n % 2):1024 * (n % 2) + ALL]).then_inc(v2_done.h, 1)
                    dve.wait_ge(v2_done.h, 5)

                @block.tensor
                def _(pe):
                    pe.wait_ge(ac_done.h, 1)
                    pe.wait_ge(vv_done.h, 3)
                    half = ALL // 2
                    for h in range(2):
                        for k in range(CHUNKS):
                            last = T_.matmul(bank(h, half), ones[:, :], cmp[:, k, h * half:(h + 1) * half],
                                             start=k == 0, stop=k == CHUNKS - 1)
                    last.then_inc(pe_done.h, 1)
                    pe.wait_ge(v2_done.h, 1)
                    for k in range(CHUNKS):
                        last = T_.transpose(PS[:, 1024 + k * P:1024 + (k + 1) * P], trep[:, k * P:(k + 1) * P], ident[:, :])
                    last.then_inc(pe_done.h, 1)
                    pe.wait_ge(vv_done.h, 5)
                    for n in range(4):
                        pe.wait_ge(v2_done.h, max(1, n))
                        for k in range(CHUNKS):
                            src = (far[:, k], stepr[:, k, 2], stepr[:, k, 5], stepr[:, k, 0])[n]
                            o = 1024 * (n % 2) + k * P
                            last = T_.transpose(PS[:, o:o + P], src, ident[:, :])
                        last.then_inc(pe2_done.h, 1)
            for s, n in ((loaded, 96), (stored, 112), (vv_done, 5), (ac_done, 1), (pe_done, 2), (pe2_done, 4),
                         (v2_done, 5), (rows_here[0], 16 * CHUNKS), (pool_gate, 1)):
                s.passed(n)

        def layernorm():
            x3, h3 = blocks(X, DIM), blocks(H, DIM)
            q3 = blocks(T2, DIM)
            m, v = small[:, 0:BLOCKS], LG[:, 0:BLOCKS]
            with nc.Block() as block:
                @block.vector
                def _(dve):
                    c = vch.on(dve)
                    c.link(V.tensor_reduce(m, x3, AX.X, ALU.add))
                    c.link(V.tensor_scalar(m, m, 1.0 / DIM, None, ALU.mult))
                    c.link(V.tensor_tensor(h3, x3, each(m, DIM), ALU.subtract))
                    c.link(V.tensor_tensor(q3, h3, h3, ALU.mult))
                    c.link(V.tensor_reduce(v, q3, AX.X, ALU.add))
                    V.tensor_scalar(v, v, 1.0 / DIM, 1e-5, ALU.mult, ALU.add).then_inc(vv_done.h, 1)
                    dve.wait_ge(ac_done.h, ac_done.at(1))
                    c.link(V.reciprocal(v, v))
                    V.tensor_tensor(h3, h3, each(v, DIM), ALU.mult).then_inc(vv_done.h, 1)

                @block.scalar
                def _(act):
                    act.wait_ge(vv_done.h, vv_done.at(1))
                    S_.activation(v, v, ACT.Sqrt).then_inc(ac_done.h, 1)
                    act.wait_ge(vv_done.h, vv_done.at(2))
                    S_.activation(H[:, :], H[:, :], ACT.Relu).then_inc(ac_done.h, 1)
            vv_done.passed(2)
            ac_done.passed(2)

        def load_weights(items):
            with nc.Block() as block:
                @block.sync
                def _(sp):
                    for at, parts, ap, *first in items:
                        p0 = first[0] if first else 0
                        sp.dma_start(W[p0:p0 + parts, at:at + ap.shape[1]], ap).then_inc(loaded.h, 16)
                    sp.wait_ge(loaded.h, loaded.at(16 * len(items)))
            loaded.passed(16 * len(items))

        wcol = lambda k, parts=P: W[0:parts, k * DIM:(k + 1) * DIM]
        bias_row = lambda ap, n=DIM: ap.rearrange("(a n) -> a n", a=1)[0:1, 0:n].to_broadcast([P, n])

        def node_linear(srcs, outs, stage):
            K = len(srcs)
            view = lambda spec, j: (spec[0][:, bass.ds(j * (NB * spec[1]), NB * spec[1])]
                                    .rearrange("p (u w) -> p u w", w=spec[1])[:, :, spec[2]:spec[2] + DIM])
            room = [stage[:, k * NB * DIM:(k + 1) * NB * DIM] for k in range(2 * K)]
            n_out = len(outs)
            with nc.Block() as block:
                @block.scalar
                def _(act):
                    with act.Fori(0, BLOCKS // NB) as j:
                        act.wait_ge(pB[0].h, pB[0].at(j * n_out + 1))
                        for k in range(K):
                            S_.activation(room[k].rearrange("p (u w) -> p u w", w=DIM), view(srcs[k], j),
                                          ACT.Copy).then_inc(aA[0].h, 1)
                        for k in range(K):
                            act.wait_ge(pA[0].h, pA[0].at(j * K + k + 1))
                            S_.activation(room[K + k], PS[:, 1024 * (k % 2):1024 * (k % 2) + NB * DIM], ACT.Copy).then_inc(aB[0].h, 1)

                @block.tensor
                def _(pe):
                    pe.sem_inc(pB[0].h, 1)
                    with pe.Fori(0, BLOCKS // NB) as j:
                        for k in range(K):
                            pe.wait_ge(aA[0].h, aA[0].at(j * K + k + 1))
                            if k >= 2:
                                pe.wait_ge(aB[0].h, aB[0].at(j * K + k - 1))
                            for u in range(NB):
                                o = 1024 * (k % 2) + u * P
                                last = T_.transpose(PS[:, o:o + P], room[k][:, u * P:(u + 1) * P], ident[:, :])
                            last.then_inc(pA[0].h, 1)
                        pe.wait_ge(aB[0].h, aB[0].at(j * K + K))
                        for n, o in enumerate(outs):
                            pe.wait_ge(v2_done.h, v2_done.at(j * n_out + n + (2 if n == 0 and n_out % 2 else 1)))
                            for u in range(NB):
                                at = 2048 + 1024 * (n % 2) + u * P
                                for k in range(K):
                                    last = T_.matmul(PS[:, at:at + P], room[K + k][:, u * P:(u + 1) * P], o["w"][k],
                                                     start=k == 0, stop=k == K - 1)
                            last.then_inc(pB[0].h, 1)

                @block.vector
                def _(dve):
                    c = vch.on(dve)
                    dve.sem_inc(v2_done.h, 2)
                    with dve.Fori(0, BLOCKS // NB) as j:
                        c.open(j, sum((o.get("plus") is not None) + bool(o.get("relu")) for o in outs))
                        for n, o in enumerate(outs):
                            at = 2048 + 1024 * (n % 2)
                            src = PS[:, at:at + NB * DIM].rearrange("p (u w) -> p u w", w=DIM)
                            to = view(o["to"], j)
                            dve.wait_ge(pB[0].h, pB[0].at(j * n_out + n + 2))
                            if o.get("plus") is not None:
                                c.link(V.tensor_tensor(to, src, view(o["plus"], j), ALU.add))
                                src = to
                            last = V.tensor_tensor(to, src, every(o["add"], NB), ALU.add)
                            if o.get("relu"):
                                c.link(last)
                                last = V.tensor_scalar(to, to, 0.0, None, ALU.max)
                            last.then_inc(v2_done.h, 1)
                    c.close(BLOCKS // NB)
            trips = BLOCKS // NB
            for s, n in ((v2_done, trips * n_out + 2), (aA[0], trips * K), (aB[0], trips * K),
                         (pA[0], trips * K), (pB[0], trips * n_out + 1)):
                s.passed(n)

        def edge_weights():
            w = LG[:, 0:STEPS]
            dup = LG[:, ALL:ALL + STEPS]
            tcols = LG[:, 2 * ALL:2 * ALL + BLOCKS]
            at = 0

            def room(n):
                nonlocal at
                at += n
                return T2[:, at - n:at]
            O8, OT8, SR8, EQ8 = (room(2 * GROUP * P) for _ in range(4))
            sg = room(TURN)
            G4 = GROUP * P
            with nc.Block() as block:
                @block.gpsimd
                def _(gp):
                    c = gch.on(gp)
                    with gp.Fori(0, TURNS) as j:
                        c.open(j, 2)
                        for g in range(2):
                            gp.wait_ge(rows_free[g].h, rows_free[g].at(j + 1))
                            c.link(G.tensor_copy(slot_idx[:, 4 * g:4 * g + 4], srci[:, bass.ds(j * TURN + 4 * g, 4)]))
                            gp.sem_inc(pool_gate.h, 1)
                            for u in range(4):
                                k = 4 * g + u
                                gp.indirect_dma_start(sg[:, k:k + 1], None, score_d[:, :], bass.IndirectOffsetOnAxis(
                                    ap=slot_idx[:, k:k + 1], axis=0)).then_inc(rows_here[g].h, 16)
                    c.close(TURNS)

                @block.sync
                def _(sp):
                    with sp.Fori(0, TURNS) as j:
                        for g in range(2):
                            sp.wait_ge(tiles_free[g].h, tiles_free[g].at(j + 1))
                            row = step_src_d[bass.ds(j * TURN + 4 * g, 4), :].rearrange("(a s) e -> a (s e)", a=1)
                            sp.dma_start(SR8[:, g * G4:(g + 1) * G4], row.to_broadcast([P, G4])).then_inc(tiles_here[g].h, 16)
                        for g in range(2):
                            sp.wait_ge(aA[g].h, aA[g].at(j + 1))
                            sp.dma_start(onehot_t_d[:, bass.ds(j * TURN * P + g * G4, G4)],
                                         OT8[:, g * G4:(g + 1) * G4]).then_inc(saved[g].h, 16)
                        for g in range(2):
                            sp.wait_ge(saved[g].h, saved[g].at(16 * j + 16))
                            sp.sem_inc(extra_free[g].h, 1)

                @block.tensor
                def _(pe):
                    with pe.Fori(0, TURNS) as j:
                        bs = [pe.value_load(brow[0:1, bass.ds(j * TURN + u, 1)], min_val=0, max_val=BLOCKS - 1) for u in range(TURN)]
                        for g in range(2):
                            pe.wait_ge(one_hots[g].h, one_hots[g].at(j + 1))
                            for u in range(4):
                                o = g * G4 + u * P
                                last = T_.transpose(bank(g)[:, u * P:(u + 1) * P], O8[:, o:o + P], ident[:, :])
                            last.then_inc(pA[g].h, 1)
                        for g in range(2):
                            pe.wait_ge(aA[g].h, aA[g].at(j + 1))
                            pe.wait_ge(vA[g].h, vA[g].at(j + 1))
                            for u in range(4):
                                o = g * G4 + u * P
                                T_.matmul(bank(2 + g)[:, u:u + 1], OT8[:, o:o + P], tcols[:, bass.ds(bs[4 * g + u], 1)], start=True, stop=True)
                                last = T_.matmul(bank(2 + g)[:, 8 + u:9 + u], O8[:, o:o + P], ones[:, 0:1], start=True, stop=True)
                            last.then_inc(pB[g].h, 1)

                @block.scalar
                def _(act):
                    with act.Fori(0, TURNS) as j:
                        for g in range(2):
                            act.wait_ge(pA[g].h, pA[g].at(j + 1))
                            act.wait_ge(extra_free[g].h, extra_free[g].at(j + 1))
                            act.wait_ge(vA[g].h, vA[g].at(j + 1))
                            S_.activation(OT8[:, g * G4:(g + 1) * G4], bank(g), ACT.Copy).then_inc(aA[g].h, 1)

                @block.vector
                def _(dve):
                    c = vch.on(dve)
                    c.link(V.memset(cnt[:, :], 0.0))
                    for g in range(2):
                        dve.sem_inc(rows_free[g].h, 1)
                        dve.sem_inc(tiles_free[g].h, 1)
                        dve.sem_inc(vA[g].h, 1)
                        dve.sem_inc(extra_free[g].h, 1)
                    with dve.Fori(0, TURNS) as j:
                        c.open(j, 4)
                        for g in range(2):
                            s0 = j * TURN + 4 * g
                            O4 = O8[:, g * G4:(g + 1) * G4].rearrange("p (u e) -> p u e", e=P)
                            V.tensor_tensor(O4, every(iota[:, :], 4), each(dloc[:, bass.ds(s0, 4)], P), ALU.is_equal).then_inc(one_hots[g].h, 1)
                        for g in range(2):
                            s0 = j * TURN + 4 * g
                            EQ = EQ8[:, g * G4:(g + 1) * G4].rearrange("p (u e) -> p u e", e=P)
                            SR = SR8[:, g * G4:(g + 1) * G4].rearrange("p (u e) -> p u e", e=P)
                            dve.wait_ge(tiles_here[g].h, tiles_here[g].at(16 * j + 16))
                            c.link(V.tensor_tensor(EQ, SR, each(srcf[:, bass.ds(s0, 4)], P), ALU.is_equal))
                            c.link(V.tensor_tensor(EQ, EQ, every(lower[:, :], 4), ALU.mult))
                            V.tensor_reduce(dup[:, bass.ds(s0, 4)], EQ, AX.X, ALU.add).then_inc(tiles_free[g].h, 1)
                        for g in range(2):
                            s0 = j * TURN + 4 * g
                            dve.wait_ge(pB[g].h, pB[g].at(j + 1))
                            dve.wait_ge(rows_here[g].h, rows_here[g].at(64 * j + 64))
                            V.tensor_tensor(w[:, bass.ds(s0, 4)], sg[:, 4 * g:4 * g + 4], bank(2 + g)[:, 0:4], ALU.add).then_inc(rows_free[g].h, 1)
                            for u in range(4):
                                b = dve.value_load(brow[0:1, bass.ds(s0 + u, 1)], min_val=0, max_val=BLOCKS - 1)
                                o = cnt[:, bass.ds(b, 1)]
                                last = V.tensor_tensor(o, o, bank(2 + g)[:, 8 + u:9 + u], ALU.add)
                                last.then_inc(vB[0].h, 1)
                                dve.wait_ge(vB[0].h, vB[0].at(j * 8 + (4 * g + u + 1)))
                            dve.sem_inc(vA[g].h, 1)
                    c.close(TURNS)
            for g in range(2):
                for s, n in ((rows_free[g], TURNS + 1), (tiles_free[g], TURNS + 1), (vA[g], TURNS + 1),
                             (extra_free[g], TURNS + 1), (saved[g], 16 * TURNS), (rows_here[g], 64 * TURNS), (tiles_here[g], 16 * TURNS),
                             (aA[g], TURNS), (pA[g], TURNS), (pB[g], TURNS), (one_hots[g], TURNS)):
                    s.passed(n)
            vB[0].passed(8 * TURNS)
            pool_gate.passed(2 * TURNS)

        def softmax_over_edges():
            w, dup, t = LG[:, 0:STEPS], LG[:, ALL:ALL + STEPS], T2[:, 0:STEPS]
            mx, ax, sm, asm_ = (small[:, k:k + 1] for k in range(4))
            with nc.Block() as block:
                @block.vector
                def _(dve):
                    c = vch.on(dve)
                    d = dloc[:, 0:STEPS]
                    c.link(V.tensor_scalar(t, d, 0.0, None, ALU.is_ge))
                    c.link(V.scalar_tensor_tensor(t, d, float(P), t, ALU.is_lt, ALU.mult))
                    c.link(V.scalar_tensor_tensor(w, w, 0.01, w, ALU.mult, ALU.max))
                    c.link(V.tensor_tensor(w, w, t, ALU.mult))
                    c.link(V.tensor_scalar(t, t, BIG, -BIG, ALU.mult, ALU.add))
                    c.link(V.tensor_tensor(w, w, t, ALU.add))
                    V.tensor_reduce(mx, w, AX.X, ALU.max).then_inc(vv_done.h, 1)
                    c.link(V.tensor_scalar(dup, dup, 1.0, None, ALU.min))
                    tr = small[:, 8:9]
                    c.link(V.tensor_scalar(tr, pcol[:, :], float(TRASH), None, ALU.add))
                    q = T2[:, ALL:ALL + STEPS]
                    c.link(V.tensor_scalar(q, srcf[:, 0:STEPS], -1.0, tr, ALU.mult, ALU.add))
                    c.link(V.tensor_tensor(q, q, dup, ALU.mult))
                    c.link(V.tensor_tensor(sidx, q, srcf[:, 0:STEPS], ALU.add))
                    dve.wait_ge(gch_done.h, gch_done.at(1))
                    V.tensor_scalar(ax, ax, -1.0, None, ALU.mult).then_inc(vv_done.h, 1)
                    dve.wait_ge(gch_done.h, gch_done.at(2))
                    c.link(V.reciprocal(asm_, asm_))
                    c.link(V.tensor_scalar(w, w, asm_, None, ALU.mult))

                @block.gpsimd
                def _(gp):
                    gp.wait_ge(vv_done.h, vv_done.at(1))
                    G.partition_all_reduce(ax, mx, P, bass.bass_isa.ReduceOp.max).then_inc(gch_done.h, 1)
                    gp.wait_ge(ac_done.h, ac_done.at(1))
                    G.partition_all_reduce(asm_, sm, P, bass.bass_isa.ReduceOp.add).then_inc(gch_done.h, 1)

                @block.scalar
                def _(act):
                    act.wait_ge(vv_done.h, vv_done.at(2))
                    S_.activation(w, w, ACT.Exp, bias=ax, accum_out=sm).then_inc(ac_done.h, 1)
            for s, n in ((vv_done, 2), (gch_done, 2), (ac_done, 1)):
                s.passed(n)

        def add_messages():
            w = LG[:, 0:STEPS]
            OT8, SR8, EQ8, MS8, OUT8 = (T2[:, k * TURN * P:(k + 1) * TURN * P] for k in range(5))
            zeros = T2[:, 5 * TURN * P + 1024:5 * TURN * P + 1024 + ROWS + P]
            G4 = GROUP * P
            quad = lambda buf, g: buf[:, g * G4:(g + 1) * G4]
            with nc.Block() as block:
                @block.sync
                def _(sp):
                    with sp.Fori(0, TURNS) as j:
                        for g in range(2):
                            sp.wait_ge(pA[g].h, pA[g].last(j))
                            sp.dma_start(quad(OT8, g), onehot_t_d[:, bass.ds(j * TURN * P + g * G4, G4)]).then_inc(tiles_here[g].h, 16)
                            sp.wait_ge(vA[g].h, vA[g].last(j))
                            row = step_src_d[bass.ds(j * TURN + 4 * g, 4), :].rearrange("(a s) e -> a (s e)", a=1)
                            sp.dma_start(quad(SR8, g), row.to_broadcast([P, G4])).then_inc(tiles_here[g].h, 16)

                @block.tensor
                def _(pe):
                    for g in range(2):
                        pA[g].start(pe)
                        pB[g].start(pe)
                    with pe.Fori(0, TURNS) as j:
                        bs = blocks_of(pe, j)
                        for g in range(2):
                            pe.wait_ge(tiles_here[g].h, tiles_here[g].at(32 * j + 32))
                            pe.wait_ge(vA[g].h, vA[g].last(j))
                            for u in range(4):
                                last = T_.matmul(bank(g)[:, u * P:(u + 1) * P], quad(OT8, g)[:, u * P:(u + 1) * P],
                                                 T1[:, bass.ds(bs[4 * g + u] * DIM, DIM)], start=True, stop=True)
                            last.then_inc(pA[g].h, 1)
                        for g in range(2):
                            pe.wait_ge(vA[g].h, vA[g].turn(j))
                            pe.wait_ge(aA[g].h, aA[g].last(j))
                            for u in range(4):
                                last = T_.matmul(bank(2 + g)[:, u * P:(u + 1) * P], quad(EQ8, g)[:, u * P:(u + 1) * P],
                                                 quad(MS8, g)[:, u * P:(u + 1) * P], start=True, stop=True)
                            last.then_inc(pB[g].h, 1)

                @block.vector
                def _(dve):
                    V.memset(zeros, 0.0).then_inc(vv_done.h, 1)
                    for g in range(2):
                        vA[g].start(dve)
                    with dve.Fori(0, TURNS) as j:
                        for g in range(2):
                            s0 = j * TURN + 4 * g
                            split = lambda buf: quad(buf, g).rearrange("p (u e) -> p u e", e=P)
                            dve.wait_ge(tiles_here[g].h, tiles_here[g].at(32 * j + 32))
                            dve.wait_ge(pB[g].h, pB[g].last(j))
                            V.tensor_tensor(split(EQ8), split(SR8), each(srcf[:, bass.ds(s0, 4)], P), ALU.is_equal)
                            dve.wait_ge(pA[g].h, pA[g].turn(j))
                            V.tensor_tensor(split(MS8), bank(g).rearrange("p (u e) -> p u e", e=P),
                                            each(w[:, bass.ds(s0, 4)], P), ALU.mult).then_inc(vA[g].h, 1)

                @block.scalar
                def _(act):
                    for g in range(2):
                        aA[g].start(act)
                    with act.Fori(0, TURNS) as j:
                        for g in range(2):
                            act.wait_ge(pB[g].h, pB[g].turn(j))
                            for u in range(4):
                                act.wait_ge(scattered[4 * g + u].h, scattered[4 * g + u].at(16 * j + 16))
                            S_.activation(quad(OUT8, g), bank(2 + g), ACT.Copy).then_inc(aA[g].h, 1)

                @block.gpsimd
                def _(gp):
                    c = gch.on(gp)
                    gp.wait_ge(vv_done.h, vv_done.at(1))
                    for k in range(COPIES):
                        gp.dma_start(added_d[k].rearrange("(t p) f -> p t f", p=P),
                                     zeros.rearrange("p (t f) -> p t f", f=DIM)).then_inc(scattered[k].h, 16)
                    with gp.Fori(0, TURNS) as j:
                        c.open(j, 2)
                        for g in range(2):
                            gp.wait_ge(aA[g].h, aA[g].turn(j))
                            c.link(G.tensor_copy(slot_idx[:, 4 * g:4 * g + 4], sidx[:, bass.ds(j * TURN + 4 * g, 4)]))
                            gp.sem_inc(pool_gate.h, 1)
                            for u in range(4):
                                k = 4 * g + u
                                gp.indirect_dma_start(added_d[k][:, :], bass.IndirectOffsetOnAxis(ap=slot_idx[:, k:k + 1], axis=0),
                                                      quad(OUT8, g)[:, u * P:(u + 1) * P], None,
                                                      compute_op=ALU.add).then_inc(scattered[k].h, 16)
                    c.close(TURNS)
                    for k in range(COPIES):
                        gp.wait_ge(scattered[k].h, scattered[k].at(16 * TURNS + 16))
            for g in range(2):
                for s, n in ((pA[g], TURNS + 1), (pB[g], TURNS + 1), (vA[g], TURNS + 1), (aA[g], TURNS + 1),
                             (tiles_here[g], 32 * TURNS)):
                    s.passed(n)
            for k in range(COPIES):
                scattered[k].passed(16 * TURNS + 16)
            vv_done.passed(1)
            pool_gate.passed(2 * TURNS)

            halves = [T1[:, 0:ROWS], T1[:, ROWS:2 * ROWS], T2[:, 0:ROWS], T2[:, ROWS:2 * ROWS]]
            with nc.Block() as block:
                @block.sync
                def _(sp):
                    for k in range(COPIES):
                        if k >= 4:
                            sp.wait_ge(vv_done.h, vv_done.at(k - 3))
                        sp.dma_start(halves[k % 4].rearrange("p (t f) -> p t f", f=DIM),
                                     added_d[k][0:ROWS, :].rearrange("(t p) f -> p t f", p=P)).then_inc(scattered_read[k].h, 16)

                @block.vector
                def _(dve):
                    for k in range(COPIES):
                        dve.wait_ge(scattered_read[k].h, 16)
                        V.tensor_tensor(X[:, :], X[:, :], halves[k % 4], ALU.add).then_inc(vv_done.h, 1)
                        dve.wait_ge(vv_done.h, vv_done.at(k + 1))
            vv_done.passed(COPIES)

        def table_to_dram(tab, width, dst):
            with nc.Block() as block:
                @block.sync
                def _(sp):
                    sp.dma_start(dst.rearrange("(t p) f -> p t f", p=P), blocks(tab, width)).then_inc(stored.h, 16)
                    sp.wait_ge(stored.h, stored.at(16))
            stored.passed(16)

        def layer0():
            load_weights([(0, P, I["L0_W_w"]), (DIM, P, bias_row(I["L0_W_b"])),
                          (2 * DIM, P, bias_row(I["L0_a_w"])), (3 * DIM, P, bias_row(I["L0_a_w2"])),
                          (4 * DIM, P, bias_row(I["L0_a_b"], 1))])
            layernorm()
            node_linear([(H, DIM, 0)], [dict(w=[wcol(0)], add=wcol(1), to=(T1, DIM, 0))], T2)
            tab, q = blocks(T1, DIM), blocks(T2, DIM)
            sc, tc = small[:, 0:BLOCKS], LG[:, 2 * ALL:2 * ALL + BLOCKS]
            with nc.Block() as block:
                @block.vector
                def _(dve):
                    c = vch.on(dve)
                    c.link(V.tensor_tensor(q, tab, every(wcol(2), BLOCKS), ALU.mult))
                    c.link(V.tensor_reduce(sc, q, AX.X, ALU.add))
                    c.link(V.tensor_tensor(q, tab, every(wcol(3), BLOCKS), ALU.mult))
                    c.link(V.tensor_reduce(tc, q, AX.X, ALU.add))
                    V.tensor_scalar(tc, tc, W[:, 4 * DIM:4 * DIM + 1], None, ALU.add).then_inc(vv_done.h, 1)

                @block.sync
                def _(sp):
                    sp.wait_ge(vv_done.h, vv_done.at(1))
                    with nc.allow_non_contiguous_dma(reason="one score per node"):
                        sp.dma_start(score_d.rearrange("(t p) a -> p t a", p=P), sc.unsqueeze(2)).then_inc(stored.h, 16)
                    sp.wait_ge(stored.h, stored.at(16))
            vv_done.passed(1)
            stored.passed(16)
            edge_weights()
            softmax_over_edges()
            add_messages()

        def gather_rows(gp, table, rows, width, free, turns=TURNS):
            c = gch.on(gp)
            with gp.Fori(0, turns) as j:
                c.open(j, 2)
                for g in range(2):
                    free(g, j)
                    c.link(G.tensor_copy(slot_idx[:, 4 * g:4 * g + 4], srci[:, bass.ds(j * TURN + 4 * g, 4)]))
                    gp.sem_inc(pool_gate.h, 1)
                    for u in range(4):
                        k = 4 * g + u
                        gp.indirect_dma_start(rows[:, k * width:(k + 1) * width], None, table[:, :],
                                              bass.IndirectOffsetOnAxis(ap=slot_idx[:, k:k + 1], axis=0)).then_inc(rows_here[g].h, 16)
            c.close(turns)

        def one_hot(buf, g, places, s0):
            return V.tensor_tensor(buf[:, g * GROUP * P:(g + 1) * GROUP * P].rearrange("p (u e) -> p u e", e=P),
                                   every(iota[:, :], 4), each(places[:, bass.ds(s0, 4)], P), ALU.is_equal)

        def add_to_table(dve, c, table, width, s0, products):
            for u in range(4):
                b = dve.value_load(brow[0:1, bass.ds(s0 + u, 1)], min_val=0, max_val=BLOCKS - 1)
                o = table[:, bass.ds(b * width, width)]
                c.link(V.tensor_tensor(o, o, products[u], ALU.add))

        quad = lambda buf, g, w=P: buf[:, g * GROUP * w:(g + 1) * GROUP * w]
        split = lambda ap, w=P: ap.rearrange("p (u e) -> p u e", e=w)
        part = lambda ap, u, w=P: ap[:, u * w:(u + 1) * w]

        def edge_mlp_sums():
            R8, O8, M8, EAT8, EA8 = (T2[:, k * TURN * P:(k + 1) * TURN * P] for k in range(5))
            with nc.Block() as block:
                @block.gpsimd
                def _(gp):
                    gather_rows(gp, gather_d, R8, DIM, lambda g, j: gp.wait_ge(vA[g].h, vA[g].last(j)))

                @block.sync
                def _(sp):
                    with sp.Fori(0, TURNS) as j:
                        for g in range(2):
                            ts = [sp.value_load(trow[0:1, bass.ds(j * TURN + 4 * g + u, 1)], min_val=0, max_val=TILES - 1) for u in range(4)]
                            sp.wait_ge(pA[g].h, pA[g].last(j))
                            for u in range(4):
                                sp.dma_start(part(quad(EA8, g, EDGE_DIM), u, EDGE_DIM),
                                             I["ea"][bass.ds(ts[u] * P, P), :]).then_inc(tiles_here[g].h, 16)

                @block.tensor
                def _(pe):
                    for g in range(2):
                        for s in (pA, pB, pC):
                            s[g].start(pe)
                    with pe.Fori(0, TURNS) as j:
                        for g in range(2):
                            pe.wait_ge(tiles_here[g].h, tiles_here[g].at(64 * j + 64))
                            pe.wait_ge(aA[g].h, aA[g].last(j))
                            for v in range(2):
                                last = T_.transpose(part(bank(g), v), part(quad(EA8, g, EDGE_DIM), v), ident[:, :])
                            last.then_inc(pA[g].h, 1)
                        for g in range(2):
                            pe.wait_ge(aA[g].h, aA[g].turn(j))
                            pe.wait_ge(vA[g].h, vA[g].last(j))
                            for u in range(4):
                                half = slice(EDGE_DIM * (u % 2), EDGE_DIM * (u % 2 + 1))
                                last = T_.matmul(part(bank((2, 6)[u % 2] + g), u // 2), part(quad(EAT8, g, EDGE_DIM), u // 2)[half], wcol(2)[half], start=True, stop=True)
                            last.then_inc(pB[g].h, 1)
                        for g in range(2):
                            pe.wait_ge(aB[g].h, aB[g].turn(j))
                            pe.wait_ge(vB[g].h, vB[g].turn(j))
                            pe.wait_ge(vC[g].h, vC[g].last(j))
                            for u in range(4):
                                last = T_.matmul(part(bank(4 + g), u), part(quad(O8, g), u), part(quad(M8, g), u), start=True, stop=True)
                            last.then_inc(pC[g].h, 1)

                @block.scalar
                def _(act):
                    for g in range(2):
                        aA[g].start(act)
                        aB[g].start(act)
                    with act.Fori(0, TURNS) as j:
                        for g in range(2):
                            act.wait_ge(pA[g].h, pA[g].turn(j))
                            act.wait_ge(pB[g].h, pB[g].last(j))
                            S_.activation(quad(EAT8, g, EDGE_DIM), bank(g, 2 * P), ACT.Copy).then_inc(aA[g].h, 1)
                        for g in range(2):
                            act.wait_ge(vA[g].h, vA[g].turn(j))
                            S_.activation(quad(M8, g), quad(M8, g), ACT.Relu).then_inc(aB[g].h, 1)

                @block.vector
                def _(dve):
                    c = vch.on(dve)
                    c.link(V.memset(T1[:, 0:ROWS], 0.0))
                    for g in range(2):
                        for s in (vA, vB, vC):
                            s[g].start(dve)
                    with dve.Fori(0, TURNS) as j:
                        c.open(j, 8)
                        for g in range(2):
                            dve.wait_ge(pC[g].h, pC[g].last(j))
                            one_hot(O8, g, dloc, j * TURN + 4 * g).then_inc(vB[g].h, 1)
                        for g in range(2):
                            dve.wait_ge(rows_here[g].h, rows_here[g].at(64 * j + 64))
                            dve.wait_ge(pB[g].h, pB[g].turn(j))
                            for half in range(2):
                                pick = lambda buf: split(quad(buf, g))[:, half::2]
                                last = V.tensor_tensor(pick(M8), split(bank((2, 6)[half] + g, 2 * P)), pick(R8), ALU.add)
                            last.then_inc(vA[g].h, 1)
                        for g in range(2):
                            dve.wait_ge(pC[g].h, pC[g].turn(j))
                            add_to_table(dve, c, T1, DIM, j * TURN + 4 * g, [part(bank(4 + g), u) for u in range(4)])
                            dve.sem_inc(vC[g].h, 1)
                    c.close(TURNS)
            for g in range(2):
                for s in (pA, pB, pC, aA, aB, vA, vB, vC):
                    s[g].passed(TURNS + 1)
                rows_here[g].passed(64 * TURNS)
                tiles_here[g].passed(64 * TURNS)
            pool_gate.passed(2 * TURNS)

        def clipped_counts(dve, c):
            c.link(V.tensor_scalar(small[:, 0:BLOCKS], cnt[:, :], 1.0, None, ALU.max))
            c.link(V.reciprocal(small[:, 0:BLOCKS], small[:, 0:BLOCKS]))
            c.link(V.tensor_scalar(has[:, :], cnt[:, :], 1.0, None, ALU.min))

        def layer1():
            layernorm()
            load_weights([(0, P, I["L1_W1a"][0:DIM, :]), (DIM, P, bias_row(I["L1_b1a"])),
                          (2 * DIM, EDGE_DIM, I["L1_W1a"][DIM:DIM + EDGE_DIM, :]),
                          (2 * DIM, EDGE_DIM, I["L1_W1a"][DIM:DIM + EDGE_DIM, :], EDGE_DIM)])
            node_linear([(H, DIM, 0)], [dict(w=[wcol(0)], add=wcol(1), to=(T1, DIM, 0))], T2)
            table_to_dram(T1, DIM, gather_d)
            edge_mlp_sums()
            w2 = I["L1_W2a"]
            load_weights([(0, P, I["L1_W1b"]), (DIM, P, bias_row(I["L1_b1b"])), (2 * DIM, P, w2[0:P, :]),
                          (3 * DIM, P, w2[P:2 * P, :]), (4 * DIM, EDGE_DIM, w2[2 * P:2 * P + EDGE_DIM, :]),
                          (5 * DIM, P, bias_row(I["L1_b2a"])), (6 * DIM, P, I["L1_W2b"]),
                          (7 * DIM, P, bias_row(I["L1_b2b"])),
                          (8 * DIM, EDGE_DIM, I["L1_u"][0:1, :].rearrange("a n -> n a"))])
            sums = blocks(T1, DIM)
            with nc.Block() as block:
                @block.vector
                def _(dve):
                    c = vch.on(dve)
                    clipped_counts(dve, c)
                    c.link(V.tensor_tensor(sums, sums, each(small[:, 0:BLOCKS], DIM), ALU.mult))
                    c.link(V.tensor_copy(W[0:EDGE_DIM, 9 * DIM:10 * DIM], W[0:EDGE_DIM, 8 * DIM:8 * DIM + 1].to_broadcast([EDGE_DIM, DIM])))
                    dve.sem_inc(vv_done.h, 1)
                    dve.wait_ge(pe_done.h, pe_done.at(1))
                    c.link(V.tensor_tensor(wcol(5), wcol(5), bank(0, DIM), ALU.add))

                @block.tensor
                def _(pe):
                    pe.wait_ge(vv_done.h, vv_done.at(1))
                    T_.matmul(bank(0, DIM), W[0:EDGE_DIM, 9 * DIM:10 * DIM], W[0:EDGE_DIM, 4 * DIM:5 * DIM],
                              start=True, stop=True).then_inc(pe_done.h, 1)
            vv_done.passed(1)
            pe_done.passed(1)
            node_linear([(T1, DIM, 0)], [dict(w=[wcol(0)], add=wcol(1), to=(T1, DIM, 0))], T2)
            with nc.Block() as block:
                @block.vector
                def _(dve):
                    c = vch.on(dve)
                    c.link(V.tensor_tensor(sums, sums, each(has[:, :], DIM), ALU.mult))
            node_linear([(H, DIM, 0), (T1, DIM, 0)],
                        [dict(w=[wcol(2), wcol(3)], add=wcol(5), relu=True, to=(T1, DIM, 0))], T2)
            node_linear([(T1, DIM, 0)], [dict(w=[wcol(6)], add=wcol(7), plus=(X, DIM, 0), to=(X, DIM, 0))], T2)

        def step_neighbours():
            rows = [T2[0:HEADS, k * ALL:(k + 1) * ALL] for k in range(4)]
            with nc.Block() as block:
                @block.sync
                def _(sp):
                    with nc.allow_non_contiguous_dma(reason="one edge of each step"):
                        for row, (s0, e) in zip(rows, ((1, P - 1), (0, P - 1), (1, 0), (2, 0))):
                            src = step_dst_d[s0:s0 + ALL, e:e + 1].rearrange("s e -> e s").to_broadcast([HEADS, ALL])
                            sp.dma_start(row, src).then_inc(loaded.h, 16)
                    sp.wait_ge(loaded.h, loaded.at(64))

                @block.vector
                def _(dve):
                    c = vch.on(dve)
                    dve.wait_ge(loaded.h, loaded.at(64))
                    for k, to in enumerate((goes_on, came_on)):
                        c.link(V.tensor_tensor(to[:, :], rows[2 * k], rows[2 * k + 1], ALU.not_equal))
                        c.link(V.tensor_scalar(to[:, :], to[:, :], -BIG, None, ALU.mult))
            loaded.passed(64)

        def edge_logits(heads, width, table, att, we):
            R8, M8 = (T1[:, k * TURN * WIDE:k * TURN * WIDE + TURN * width] for k in range(2))
            OT8 = T1[:, 4 * TURN * P:5 * TURN * P]
            per_bank = 512 // width
            spot = lambda g, u: PS[:, 2048 * g + u // per_bank * 512 + u % per_bank * width:][:, 0:width]
            W4 = GROUP * width
            kept = edge_rows_d[:, 0:STEPS * width]
            with nc.Block() as block:
                @block.gpsimd
                def _(gp):
                    def free(g, j):
                        gp.wait_ge(pA[g].h, pA[g].last(j))
                        gp.sem_inc(pool_gate.h, 1)
                        gp.wait_ge(aA[g].h, aA[g].last(j))
                    gather_rows(gp, table, R8, width, free)

                @block.sync
                def _(sp):
                    with sp.Fori(0, TURNS) as j:
                        for g in range(2):
                            sp.wait_ge(pA[g].h, pA[g].last(j))
                            sp.dma_start(quad(OT8, g), onehot_t_d[:, bass.ds(j * TURN * P + g * GROUP * P, GROUP * P)]).then_inc(tiles_here[g].h, 16)

                @block.scalar
                def _(act):
                    for g in range(2):
                        aA[g].start(act)
                    with act.Fori(0, TURNS) as j:
                        for g in range(2):
                            act.wait_ge(rows_here[g].h, rows_here[g].at(64 * j + 64))
                            act.dma_start(kept[:, bass.ds(j * TURN * width + g * W4, W4)], quad(R8, g, width)).then_inc(saved[g].h, 16)
                        for g in range(2):
                            act.wait_ge(saved[g].h, saved[g].at(16 * j + 16))
                            act.sem_inc(aA[g].h, 1)

                @block.tensor
                def _(pe):
                    for g in range(2):
                        pA[g].start(pe)
                    with pe.Fori(0, TURNS) as j:
                        bs = blocks_of(pe, j)
                        for g in range(2):
                            pe.wait_ge(tiles_here[g].h, tiles_here[g].at(16 * j + 16))
                            pe.wait_ge(rows_here[g].h, rows_here[g].at(64 * j + 64))
                            pe.wait_ge(vA[g].h, vA[g].last(j))
                            for u in range(4):
                                T_.matmul(spot(g, u), part(quad(OT8, g), u), T2[:, bass.ds(bs[4 * g + u] * width, width)], start=True, stop=False)
                                last = T_.matmul(spot(g, u), ident[:, :], part(quad(R8, g, width), u, width), start=False, stop=True)
                            last.then_inc(pA[g].h, 1)

                @block.vector
                def _(dve):
                    c = vch.on(dve)
                    c.link(V.memset(LG[:, :], 0.0))
                    for g in range(2):
                        vA[g].start(dve)
                    with dve.Fori(0, TURNS) as j:
                        c.open(j, 4)
                        for g in range(2):
                            s0 = j * TURN + 4 * g
                            m = quad(M8, g, width)
                            dve.wait_ge(pA[g].h, pA[g].turn(j))
                            for u in range(4):
                                last = V.scalar_tensor_tensor(part(m, u, width), we, ew[:, bass.ds(s0 + u, 1)], spot(g, u), ALU.mult, ALU.add)
                            last.then_inc(vA[g].h, 1)
                            dve.wait_ge(vA[g].h, vA[g].turn(j))
                            c.link(V.scalar_tensor_tensor(m, m, 0.2, m, ALU.mult, ALU.max))
                            c.link(V.tensor_tensor(split(m, width), split(m, width), every(att, 4), ALU.mult))
                            V.tensor_reduce(LG[:, bass.ds(s0 * heads, 4 * heads)], split(m, width // heads), AX.X, ALU.add)
                    c.close(TURNS)
            for g in range(2):
                for s in (pA, aA, vA):
                    s[g].passed(TURNS + 1)
                rows_here[g].passed(64 * TURNS)
                tiles_here[g].passed(16 * TURNS)
                saved[g].passed(16 * TURNS)
            pool_gate.passed(4 * TURNS)

        def segment_weights(heads):
            n = CHUNKS * heads * P
            L, F, B = (T1[:, k * 3584:k * 3584 + n] for k in range(3))
            mask = T2[:, 0:n]
            dst_r, mf, mb, eq, tmp, valid = (T2[:, 3584 + k * ALL:3584 + (k + 1) * ALL] for k in range(6))
            rowF, rowB = (T2[0:heads, 3584 + (6 + k) * ALL:3584 + (7 + k) * ALL] for k in range(2))
            k0 = 3584 + 8 * ALL
            prev, nxt = T2[:, k0:k0 + CHUNKS], T2[:, k0 + 8:k0 + 8 + CHUNKS]
            eF, eB, cF, cB = (T2[:, k0 + 16 + 32 * k:k0 + 16 + 32 * k + CHUNKS * heads] for k in range(4))
            nobody = T2[0:heads, k0 + 144:k0 + 145]
            che = lambda ap: ap.rearrange("p (c h e) -> p c h e", h=heads, e=P)
            ce = lambda ap: ap.rearrange("p (c e) -> p c e", e=P)
            ch = lambda ap: ap.rearrange("p (c h) -> p c h", h=heads)
            lgs = LG[:, 0:ALL * heads].rearrange("p (s h) -> p s h", h=heads)
            rows_of = lambda d: d.rearrange("(c p) e -> p c e", p=P)
            ends = lambda d, o: d[0:heads, o:o + ALL].rearrange("h (c p) -> p h c", p=P)
            with nc.Block() as block:
                @block.sync
                def _(sp):
                    sp.dma_start(ce(dst_r), rows_of(step_dst_d[1:ALL + 1, :])).then_inc(loaded.h, 16)
                    sp.dma_start(ce(mf), rows_of(step_first_d)).then_inc(loaded.h, 16)
                    sp.dma_start(ce(mb), rows_of(step_last_d)).then_inc(loaded.h, 16)
                    with nc.allow_non_contiguous_dma(reason="one number of each step"):
                        sp.dma_start(prev.unsqueeze(2), rows_of(step_dst_d[0:ALL, P - 1:P])).then_inc(loaded.h, 16)
                        sp.dma_start(nxt.unsqueeze(2), rows_of(step_dst_d[2:ALL + 2, 0:1])).then_inc(loaded.h, 16)
                        sp.wait_ge(vv_done.h, vv_done.at(2))
                        for h in range(heads):
                            for d, e in ((ends_d, eF), (ends2_d, eB)):
                                sp.dma_start(d[h:h + 1, 1:ALL + 1].rearrange("a (c p) -> p c a", p=P), ch(e)[:, :, h:h + 1]).then_inc(stored.h, 16)
                        sp.wait_ge(stored.h, stored.at(32 * heads))
                        sp.dma_start(rowF, ends_d[0:heads, 1:ALL + 1]).then_inc(loaded.h, 16)
                        sp.dma_start(rowB, ends2_d[0:heads, 1:ALL + 1]).then_inc(loaded.h, 16)
                        sp.wait_ge(vv_done.h, vv_done.at(3))
                        for d, row in ((ends_d, rowF), (ends2_d, rowB)):
                            sp.dma_start(d[0:heads, 1:ALL + 1], row).then_inc(stored.h, 16)
                            sp.dma_start(d[0:heads, 0:1], nobody).then_inc(stored.h, 16)
                            sp.dma_start(d[0:heads, ALL + 1:ALL + 2], nobody).then_inc(stored.h, 16)
                        sp.wait_ge(stored.h, stored.at(32 * heads + 96))
                        for h in range(heads):
                            for d, o, cc in ((ends_d, 0, cF), (ends2_d, 2, cB)):
                                sp.dma_start(ch(cc)[:, :, h:h + 1], d[h:h + 1, o:o + ALL].rearrange("a (c p) -> p c a", p=P)).then_inc(loaded.h, 16)
                    sp.wait_ge(loaded.h, loaded.at(16 * 7 + 32 * heads))

                @block.vector
                def _(dve):
                    c = vch.on(dve)
                    c.link(V.tensor_scalar(valid, dloc[:, :], 0.0, None, ALU.is_ge))
                    c.link(V.scalar_tensor_tensor(valid, dloc[:, :], float(P), valid, ALU.is_lt, ALU.mult))
                    V.memset(nobody, -BIG)
                    c.link(V.tensor_scalar(tmp, valid, BIG, -BIG, ALU.mult, ALU.add))
                    c.link(V.tensor_tensor(lgs, lgs, each(valid, heads), ALU.mult))
                    V.tensor_tensor(lgs, lgs, each(tmp, heads), ALU.add).then_inc(vv_done.h, 1)
                    dve.wait_ge(loaded.h, loaded.at(80))
                    dve.wait_ge(ac_done.h, ac_done.at(1))
                    for src, edge, to, way in ((mf, 0, F, 1), (mb, P - 1, B, -1)):
                        for h in range(heads):
                            c.link(V.tensor_copy(che(mask)[:, :, h], ce(src)))
                        c.link(V.memset(che(mask)[:, :, :, edge], -BIG))
                        c.link(V.tensor_tensor_scan(to[:, ::way], mask[:, ::way], L[:, ::way], -BIG, ALU.add, ALU.max))
                    c.link(V.tensor_tensor(F, F, B, ALU.max))
                    c.link(V.tensor_copy(ch(eF), che(F)[:, :, :, P - 1]))
                    V.tensor_copy(ch(eB), che(F)[:, :, :, 0]).then_inc(vv_done.h, 1)
                    dve.wait_ge(loaded.h, loaded.at(112))
                    c.link(V.tensor_tensor_scan(T1[0:heads, 7168:7168 + ALL], goes_on[0:heads, :], rowF, -BIG, ALU.add, ALU.max))
                    c.link(V.tensor_tensor_scan(T1[0:heads, 7168 + ALL:7168 + 2 * ALL][:, ::-1], came_on[0:heads, ::-1], rowB[:, ::-1], -BIG, ALU.add, ALU.max))
                    c.link(V.tensor_copy(rowF, T1[0:heads, 7168:7168 + ALL]))
                    V.tensor_copy(rowB, T1[0:heads, 7168 + ALL:7168 + 2 * ALL]).then_inc(vv_done.h, 1)
                    dve.wait_ge(loaded.h, loaded.at(16 * 7 + 32 * heads))
                    for border, carry in ((prev, cF), (nxt, cB)):
                        c.link(V.tensor_tensor(ce(eq), ce(dst_r), each(border, P), ALU.is_equal))
                        c.link(V.tensor_scalar(eq, eq, BIG, -BIG, ALU.mult, ALU.add))
                        for h in range(heads):
                            c.link(V.tensor_tensor(ce(tmp), ce(eq), each(ch(carry)[:, :, h], P), ALU.add))
                            c.link(V.tensor_tensor(che(F)[:, :, h], che(F)[:, :, h], ce(tmp), ALU.max))
                    dve.sem_inc(vv_done.h, 1)
                    dve.wait_ge(pe_done.h, pe_done.at(2))
                    back = PS[:, 0:n].rearrange("p (c h s) -> p c h s", h=heads, s=P)
                    lgc = LG[:, 0:ALL * heads].rearrange("p (c s h) -> p c s h", s=P, h=heads)
                    for h in range(heads):
                        last = V.tensor_tensor(lgc[:, :, :, h], lgc[:, :, :, h], back[:, :, h], ALU.subtract)
                    last.then_inc(vv_done.h, 1)
                    dve.wait_ge(ac_done.h, ac_done.at(2))
                    c.link(V.tensor_tensor(lgs, lgs, each(valid, heads), ALU.mult))

                @block.tensor
                def _(pe):
                    pe.wait_ge(vv_done.h, vv_done.at(1))
                    for k in range(CHUNKS):
                        for h in range(heads):
                            o = (k * heads + h) * P
                            last = T_.transpose(PS[:, o:o + P], lgs[:, k * P:(k + 1) * P, h], ident[:, :])
                    last.then_inc(pe_done.h, 1)
                    pe.wait_ge(vv_done.h, vv_done.at(4))
                    for k in range(CHUNKS * heads):
                        last = T_.transpose(PS[:, k * P:(k + 1) * P], F[:, k * P:(k + 1) * P], ident[:, :])
                    last.then_inc(pe_done.h, 1)

                @block.scalar
                def _(act):
                    act.wait_ge(pe_done.h, pe_done.at(1))
                    S_.activation(L, PS[:, 0:n], ACT.Copy).then_inc(ac_done.h, 1)
                    act.wait_ge(vv_done.h, vv_done.at(5))
                    S_.activation(LG[:, 0:ALL * heads], LG[:, 0:ALL * heads], ACT.Exp).then_inc(ac_done.h, 1)
            for s, k in ((loaded, 112 + 32 * heads), (stored, 32 * heads + 96), (vv_done, 5), (pe_done, 2), (ac_done, 2)):
                s.passed(k)

        def weighted_sums(heads, width):
            both = width + heads
            R8, M8 = (T2[:, k * TURN * WIDE:k * TURN * WIDE + TURN * width] for k in range(2))
            O8 = T2[:, 4 * TURN * P:5 * TURN * P]
            W4 = GROUP * width
            kept = edge_rows_d[:, 0:STEPS * width]
            with nc.Block() as block:
                @block.sync
                def _(sp):
                    with sp.Fori(0, TURNS) as j:
                        for g in range(2):
                            sp.wait_ge(vA[g].h, vA[g].last(j))
                            sp.dma_start(quad(R8, g, width), kept[:, bass.ds(j * TURN * width + g * W4, W4)]).then_inc(tiles_here[g].h, 16)

                @block.tensor
                def _(pe):
                    for g in range(2):
                        pA[g].start(pe)
                    with pe.Fori(0, TURNS) as j:
                        for g in range(2):
                            pe.wait_ge(vA[g].h, vA[g].turn(j))
                            pe.wait_ge(vB[g].h, vB[g].last(j))
                            for u in range(4):
                                o = part(quad(O8, g), u)
                                T_.matmul(bank(4 * g + u, width), o, part(quad(M8, g, width), u, width), start=True, stop=True)
                                last = T_.matmul(bank(4 * g + u, both)[:, width:both], o,
                                                 LG[:, bass.ds((j * TURN + 4 * g + u) * heads, heads)], start=True, stop=True)
                            last.then_inc(pA[g].h, 1)

                @block.vector
                def _(dve):
                    c = vch.on(dve)
                    c.link(V.memset(T1[:, 0:BLOCKS * both], 0.0))
                    for g in range(2):
                        vA[g].start(dve)
                        vB[g].start(dve)
                    with dve.Fori(0, TURNS) as j:
                        c.open(j, 8)
                        for g in range(2):
                            s0 = j * TURN + 4 * g
                            dve.wait_ge(tiles_here[g].h, tiles_here[g].at(16 * j + 16))
                            dve.wait_ge(pA[g].h, pA[g].last(j))
                            one_hot(O8, g, dloc, s0)
                            w = width // heads
                            V.tensor_tensor(split(quad(M8, g, width), w), split(quad(R8, g, width), w),
                                            each(LG[:, bass.ds(s0 * heads, 4 * heads)], w), ALU.mult).then_inc(vA[g].h, 1)
                        for g in range(2):
                            dve.wait_ge(pA[g].h, pA[g].turn(j))
                            add_to_table(dve, c, T1, both, j * TURN + 4 * g, [bank(4 * g + u, both) for u in range(4)])
                            dve.sem_inc(vB[g].h, 1)
                    c.close(TURNS)
            for g in range(2):
                for s in (pA, vA, vB):
                    s[g].passed(TURNS + 1)
                tiles_here[g].passed(16 * TURNS)

        def norm_prelu(heads, width, col):
            both = width + heads
            y, z = blocks(T2, width), blocks(T1, width)
            num = blocks(T1, both)
            rden = LG[:, 0:BLOCKS * heads].rearrange("p (t h) -> p t h", h=heads)
            cb, gamma, beta = (W[:, col + k * width:col + (k + 1) * width] for k in range(3))
            tot = LG[:, 1024:1024 + width]
            scale = LG[:, 1536:1536 + width]
            real = small[:, 50:51]
            left = NODES - (BLOCKS - 1) * P
            pa = pa_col[:, 0:1]

            def totals(dve, c, tab, ready, passed):
                c.link(V.tensor_reduce(scale, tab.rearrange("p t f -> p f t"), AX.X, ALU.add))
                dve.sem_inc(vv_done.h, 1)
                dve.wait_ge(pe_done.h, pe_done.at(ready))
                c.link(V.tensor_scalar(tot, bank(0, width), 1.0 / NODES, None, ALU.mult))

            with nc.Block() as block:
                @block.vector
                def _(dve):
                    c = vch.on(dve)
                    c.link(V.tensor_scalar(real, pcol[:, :], float(left), None, ALU.is_lt))
                    c.link(V.tensor_scalar(rden, num[:, :, width:both], 1e-16, None, ALU.add))
                    c.link(V.reciprocal(LG[:, 0:BLOCKS * heads], LG[:, 0:BLOCKS * heads]))
                    w = width // heads
                    for h in range(heads):
                        c.link(V.tensor_tensor(y[:, :, h * w:(h + 1) * w], num[:, :, h * w:(h + 1) * w], each(rden[:, :, h], w), ALU.mult))
                    c.link(V.tensor_tensor(y, y, every(cb, BLOCKS), ALU.add))
                    c.link(V.tensor_scalar(y[:, BLOCKS - 1], y[:, BLOCKS - 1], real, None, ALU.mult))
                    totals(dve, c, y, 1, 1)
                    c.link(V.tensor_tensor(y, y, every(tot, BLOCKS), ALU.subtract))
                    c.link(V.tensor_scalar(y[:, BLOCKS - 1], y[:, BLOCKS - 1], real, None, ALU.mult))
                    c.link(V.tensor_tensor(z, y, y, ALU.mult))
                    totals(dve, c, z, 2, 2)
                    V.tensor_scalar(tot, tot, 1e-5, None, ALU.add).then_inc(vv_done.h, 1)
                    dve.wait_ge(ac_done.h, ac_done.at(1))
                    c.link(V.reciprocal(scale, tot))
                    c.link(V.tensor_tensor(scale, scale, gamma, ALU.mult))
                    c.link(V.tensor_tensor(y, y, every(scale, BLOCKS), ALU.mult))
                    c.link(V.tensor_tensor(y, y, every(beta, BLOCKS), ALU.add))
                    c.link(V.tensor_scalar(z, y, 0.0, pa, ALU.min, ALU.mult))
                    c.link(V.scalar_tensor_tensor(y, y, 0.0, z, ALU.max, ALU.add))

                @block.tensor
                def _(pe):
                    for k in range(2):
                        pe.wait_ge(vv_done.h, vv_done.at(k + 1))
                        T_.matmul(bank(0, width), ones[:, :], scale, start=True, stop=True).then_inc(pe_done.h, 1)

                @block.scalar
                def _(act):
                    act.wait_ge(vv_done.h, vv_done.at(3))
                    S_.activation(tot, tot, ACT.Sqrt).then_inc(ac_done.h, 1)
            vv_done.passed(3)
            pe_done.passed(2)
            ac_done.passed(1)

        def layer2():
            step_neighbours()
            layernorm()
            row = lambda name, c0=0: I[name][c0:c0 + DIM]
            halves = lambda name, at: [(at + k * DIM, P, I[name][:, k * DIM:(k + 1) * DIM]) for k in range(2)]
            load_weights(halves("L2_Wl1", 0) + halves("L2_Wr1", 2 * DIM) + [
                (4 * DIM, P, bias_row(I["L2_bl1"], WIDE)), (6 * DIM, P, bias_row(I["L2_br1"], WIDE))])
            node_linear([(H, DIM, 0)], [dict(w=[wcol(k)], add=wcol(4 + k), to=(T1, WIDE, k * DIM)) for k in range(2)], T2)
            table_to_dram(T1, WIDE, wide_d)
            node_linear([(H, DIM, 0)], [dict(w=[wcol(2 + k)], add=wcol(6 + k), to=(T2, WIDE, k * DIM)) for k in range(2)], T1)
            flat = lambda ap: ap.rearrange("h c -> (h c)")
            load_weights([(0, P, bias_row(flat(I["L2_att1"]), WIDE)), (2 * DIM, P, bias_row(flat(I["L2_We1"]), WIDE))])
            edge_logits(HEADS, WIDE, wide_d, W[:, 0:WIDE], W[:, WIDE:2 * WIDE])
            segment_weights(HEADS)
            weighted_sums(HEADS, WIDE)
            load_weights([(k * WIDE, P, bias_row(I[n], WIDE)) for k, n in enumerate(("L2_cb1", "L2_bng1", "L2_bnb1"))])
            with nc.Block() as block:
                @block.sync
                def _(sp):
                    sp.dma_start(pa_col[:, :], bias_row(I["L2_pa"], 1)).then_inc(loaded.h, 16)
                    sp.wait_ge(loaded.h, loaded.at(16))
            loaded.passed(16)
            norm_prelu(HEADS, WIDE, 0)
            load_weights([((2 * k + i) * DIM, P, I[n][i * P:(i + 1) * P, :]) for k, n in enumerate(("L2_Wl2", "L2_Wr2")) for i in range(2)]
                         + [(4 * DIM, P, bias_row(I["L2_bl2"])), (5 * DIM, P, bias_row(I["L2_br2"]))])
            node_linear([(T2, WIDE, 0), (T2, WIDE, DIM)],
                        [dict(w=[wcol(0), wcol(1)], add=wcol(4), to=(T1, DIM, 0)),
                         dict(w=[wcol(2), wcol(3)], add=wcol(5), to=(T1[:, ROWS:2 * ROWS], DIM, 0))], LG)
            table_to_dram(T1, DIM, gather_d)
            with nc.Block() as block:
                @block.scalar
                def _(act):
                    S_.activation(T2[:, 0:ROWS], T1[:, ROWS:2 * ROWS], ACT.Copy)
            load_weights([(0, P, bias_row(flat(I["L2_att2"]))), (DIM, P, bias_row(flat(I["L2_We2"])))])
            edge_logits(1, DIM, gather_d, wcol(0), wcol(1))
            segment_weights(1)
            weighted_sums(1, DIM)
            load_weights([(k * DIM, P, bias_row(I[n])) for k, n in enumerate(("L2_cb2", "L2_bng2", "L2_bnb2"))])
            norm_prelu(1, DIM, 0)
            load_weights([(0, P, I["L2_skipW"]), (DIM, P, bias_row(I["L2_skipb"]))])
            node_linear([(H, DIM, 0)], [dict(w=[wcol(0)], add=wcol(1), plus=(X, DIM, 0), to=(X, DIM, 0))], T1)
            with nc.Block() as block:
                @block.vector
                def _(dve):
                    c = vch.on(dve)
                    c.link(V.tensor_tensor(X[:, :], X[:, :], T2[:, 0:ROWS], ALU.add))

        def edge_maxima():
            R8, M8, RT8, SC8, ST8, O8, OT8, MK8 = (T2[:, k * TURN * P:(k + 1) * TURN * P] for k in range(8))
            w2 = wcol(2)
            maxima = T1[:, ROWS:2 * ROWS]
            with nc.Block() as block:
                @block.gpsimd
                def _(gp):
                    gather_rows(gp, gather_d, R8, DIM, lambda g, j: gp.wait_ge(vA[g].h, vA[g].last(j)))

                @block.sync
                def _(sp):
                    with sp.Fori(0, TURNS) as j:
                        for g in range(2):
                            sp.wait_ge(pA[g].h, pA[g].last(j))
                            sp.dma_start(quad(OT8, g), onehot_t_d[:, bass.ds(j * TURN * P + g * GROUP * P, GROUP * P)]).then_inc(tiles_here[g].h, 16)
                            sp.wait_ge(vB[g].h, vB[g].last(j))
                            row = step_first_d[bass.ds(j * TURN + 4 * g, 4), :].rearrange("(a s) e -> a (s e)", a=1)
                            sp.dma_start(quad(MK8, g), row.to_broadcast([P, GROUP * P])).then_inc(extra_here[g].h, 16)

                @block.tensor
                def _(pe):
                    for g in range(2):
                        for s in (pA, pB, pC, pD, pE):
                            s[g].start(pe)
                    with pe.Fori(0, TURNS) as j:
                        bs = blocks_of(pe, j)
                        for g in range(2):
                            pe.wait_ge(tiles_here[g].h, tiles_here[g].at(16 * j + 16))
                            pe.wait_ge(vD[g].h, vD[g].last(j))
                            for u in range(4):
                                last = T_.matmul(part(bank(g), u), part(quad(OT8, g), u), T1[:, bass.ds(bs[4 * g + u] * DIM, DIM)], start=True, stop=True)
                            last.then_inc(pA[g].h, 1)
                        for g in range(2):
                            pe.wait_ge(vA[g].h, vA[g].turn(j))
                            pe.wait_ge(aA[g].h, aA[g].last(j))
                            for u in range(4):
                                last = T_.transpose(part(bank(2 + g), u), part(quad(M8, g), u), ident[:, :])
                            last.then_inc(pB[g].h, 1)
                        for g in range(2):
                            pe.wait_ge(aA[g].h, aA[g].turn(j))
                            pe.wait_ge(vB[g].h, vB[g].last(j))
                            T_.matmul(bank(4 + g), w2, quad(RT8, g), start=True, stop=True).then_inc(pC[g].h, 1)
                        for g in range(2):
                            pe.wait_ge(vB[g].h, vB[g].turn(j))
                            pe.wait_ge(aB[g].h, aB[g].last(j))
                            for u in range(4):
                                last = T_.transpose(part(bank(6 + g), u), part(quad(SC8, g), u), ident[:, :])
                            last.then_inc(pD[g].h, 1)
                        for g in range(2):
                            pe.wait_ge(aB[g].h, aB[g].turn(j))
                            pe.wait_ge(vC[g].h, vC[g].turn(j))
                            for u in range(4):
                                last = T_.matmul(part(bank(g), u), part(quad(O8, g), u), part(quad(ST8, g), u), start=True, stop=True)
                            last.then_inc(pE[g].h, 1)

                @block.scalar
                def _(act):
                    for g in range(2):
                        aA[g].start(act)
                        aB[g].start(act)
                    with act.Fori(0, TURNS) as j:
                        for g in range(2):
                            act.wait_ge(pB[g].h, pB[g].turn(j))
                            act.wait_ge(pC[g].h, pC[g].last(j))
                            S_.activation(quad(RT8, g), bank(2 + g), ACT.Relu).then_inc(aA[g].h, 1)
                        for g in range(2):
                            act.wait_ge(pD[g].h, pD[g].turn(j))
                            act.wait_ge(pE[g].h, pE[g].last(j))
                            S_.activation(quad(ST8, g), bank(6 + g), ACT.Copy).then_inc(aB[g].h, 1)

                @block.vector
                def _(dve):
                    c = vch.on(dve)
                    V.memset(SC8, -BIG)
                    c.link(V.memset(maxima, 0.0))
                    for g in range(2):
                        for s in (vA, vB, vC, vD):
                            s[g].start(dve)
                    with dve.Fori(0, TURNS) as j:
                        c.open(j, 8)
                        for g in range(2):
                            dve.wait_ge(rows_here[g].h, rows_here[g].at(64 * j + 64))
                            dve.wait_ge(pA[g].h, pA[g].turn(j))
                            dve.wait_ge(pB[g].h, pB[g].last(j))
                            V.tensor_tensor(quad(M8, g), bank(g), quad(R8, g), ALU.add).then_inc(vA[g].h, 1)
                        for g in range(2):
                            dve.wait_ge(pE[g].h, pE[g].last(j))
                            one_hot(O8, g, dend, j * TURN + 4 * g).then_inc(vC[g].h, 1)
                        for g in range(2):
                            dve.wait_ge(extra_here[g].h, extra_here[g].at(16 * j + 16))
                            dve.wait_ge(pC[g].h, pC[g].turn(j))
                            dve.wait_ge(pD[g].h, pD[g].last(j))
                            before = 1 - g
                            dve.wait_ge(vB[before].h, vB[before].turn(j) if g else vB[before].last(j))
                            V.tensor_tensor_scan(quad(SC8, g), quad(MK8, g), bank(4 + g), quad(SC8, before)[:, GROUP * P - 1:GROUP * P],
                                                 ALU.add, ALU.max).then_inc(vB[g].h, 1)
                        for g in range(2):
                            dve.wait_ge(pE[g].h, pE[g].turn(j))
                            add_to_table(dve, c, maxima, DIM, j * TURN + 4 * g, [part(bank(g), u) for u in range(4)])
                            dve.sem_inc(vD[g].h, 1)
                    c.close(TURNS)
            for g in range(2):
                for s in (pA, pB, pC, pD, pE, aA, aB, vA, vB, vC, vD):
                    s[g].passed(TURNS + 1)
                rows_here[g].passed(64 * TURNS)
                tiles_here[g].passed(16 * TURNS)
                extra_here[g].passed(16 * TURNS)
            pool_gate.passed(2 * TURNS)

        def layer3():
            layernorm()
            for n, name in enumerate(("in", "hid", "out")):
                w1 = I[f"L3_W1_{name}"]
                load_weights([(0, P, w1[0:DIM, :]), (DIM, P, w1[DIM:2 * DIM, :]), (2 * DIM, P, I[f"L3_W2_{name}"]),
                              (3 * DIM, P, bias_row(I[f"L3_b1_{name}"])), (4 * DIM, P, bias_row(I[f"L3_b2_{name}"]))])
                with nc.Block() as block:
                    @block.vector
                    def _(dve):
                        c = vch.on(dve)
                        c.link(V.tensor_tensor(wcol(0), wcol(0), wcol(1), ALU.subtract))
                        c.link(V.memset(wcol(5), 0.0))
                node_linear([(H, DIM, 0)], [dict(w=[wcol(0)], add=wcol(3), to=(T1, DIM, 0)),
                                            dict(w=[wcol(1)], add=wcol(5), to=(T1[:, ROWS:2 * ROWS], DIM, 0))], T2)
                table_to_dram(T1[:, ROWS:2 * ROWS], DIM, gather_d)
                edge_maxima()
                m, h = blocks(T1[:, ROWS:2 * ROWS], DIM), blocks(H, DIM)
                with nc.Block() as block:
                    @block.vector
                    def _(dve):
                        c = vch.on(dve)
                        c.link(V.tensor_tensor(m, m, every(wcol(4), BLOCKS), ALU.add))
                        c.link(V.tensor_tensor(m, m, each(has[:, :], DIM), ALU.mult))
                        if n < 2:
                            c.link(V.tensor_scalar(h, m, 0.0, None, ALU.max))
                        else:
                            c.link(V.tensor_tensor(X[:, :], X[:, :], T1[:, ROWS:2 * ROWS], ALU.add))

        def give_back():
            with nc.Block() as block:
                @block.sync
                def _(sp):
                    full = NODES // P
                    sp.dma_start(out[0:full * P, :].rearrange("(t p) f -> p t f", p=P), blocks(X, DIM)[:, 0:full]).then_inc(stored.h, 16)
                    sp.dma_start(out[full * P:NODES, :], X[0:NODES - full * P, full * DIM:BLOCKS * DIM]).then_inc(stored.h, 16)
                    sp.wait_ge(stored.h, stored.at(32))
            stored.passed(32)

        setup()
        layers = [layer0, layer1, layer2, layer3] if stop > 3 else [layer0, layer1, layer2][:stop] if stop > 2 else [layer0, layer1]
        for layer in layers[:stop]:
            layer()
        give_back()


def kernel(**inputs):
    import concourse.bacc as bacc
    from concourse.bass_utils import run_bass_kernel_spmd as run

    a = {k: np.asarray(v) for k, v in inputs.items()}

    def filled(v, shape, fill, at=0):
        r = np.full(shape, fill, v.dtype)
        r[at:at + v.shape[0]] = v
        return r

    arrays = {
        "x": filled(a["x"], (ROWS, DIM), 0),
        "src": filled(a["src"], (ALL * P,), 0),
        "dst": filled(a["dst"], (ALL * P + 2,), 1 << 20, 1),
        "ew": filled(a["edge_weight1"].reshape(-1), (ALL * P,), 0),
        "ea": filled(a["edge_attr_64"], (TILES * P, EDGE_DIM), 0),
    }
    arrays["dst"][0] = -1
    for k, v in a.items():
        if k.startswith("L"):
            arrays[k.replace("_gnn_", "_")] = v.reshape(-1) if v.ndim == 0 or k == "L0_gnn_a_w" else v
    arrays["L0_a_w2"] = arrays["L0_a_w"][DIM:]
    arrays["L0_a_w"] = arrays["L0_a_w"][:DIM]
    arrays = {k: np.ascontiguousarray(v) for k, v in arrays.items()}
    nc = bacc.Bacc("TRN2", target_bir_lowering=False, num_devices=1)
    ins = {k: nc.dram_tensor(f"in_{k}", v.shape, mybir.dt.from_np(v.dtype), kind="ExternalInput").ap()
           for k, v in arrays.items()}
    out = nc.dram_tensor("out", (NODES, DIM), FP32, kind="ExternalOutput").ap()
    build(nc, ins, out, 4)
    got = run(nc, [{f"in_{k}": v for k, v in arrays.items()}], core_ids=[0])
    return got.results[0]["out"]
```

```python
from contextlib import ExitStack

import numpy as np

import concourse.bass as bass
from concourse import mybir

FP32, I32 = mybir.dt.float32, mybir.dt.int32
ALU, ACT, AX = mybir.AluOpType, mybir.ActivationFunctionType, mybir.AxisListType

P = 128
NODES, EDGES, DIM, EDGE_DIM = 6250, 100000, 128, 64
BLOCKS = -(-NODES // P)
ROWS = BLOCKS * P
TILES = -(-EDGES // P)
GROUP, TURN = 4, 8
LEAD = TURN
TURNS = -(-(LEAD + TILES + BLOCKS - 1) // TURN)
STEPS = (TURNS + 1) * TURN
CHUNKS = -(-STEPS // P)
ALL = CHUNKS * P
NB = 7
HEADS, HID = 4, 64
WIDE = HEADS * HID
FAR = float(1 << 20)
BIG = 1.0e30
COPIES = 8
TRASH = ROWS


class Signal:

    def __init__(self, handle):
        self.h, self.base = handle, 0

    def at(self, n):
        return n + self.base

    def start(self, eng):
        eng.sem_inc(self.h, 1)

    def turn(self, j):
        return j + (self.base + 2)

    def last(self, j):
        return j + (self.base + 1)

    def before(self, j):
        return j + self.base

    def passed(self, n):
        self.base += n


class Chain:

    def __init__(self, signal):
        self.s, self.k, self.j, self.per, self.eng = signal, 0, None, 0, None

    def on(self, eng):
        self.eng = eng
        return self

    def open(self, j, per):
        self.s.passed(self.k)
        self.k, self.j, self.per = 0, j, per

    def close(self, trips):
        assert self.k == self.per, (self.k, self.per)
        self.s.passed(self.per * trips)
        self.k, self.j = 0, None

    def link(self, ins, running=0):
        ins.then_inc(self.s.h, 1)
        self.k += 1
        n = self.s.at(self.k - running)
        self.eng.wait_ge(self.s.h, n if self.j is None else self.j * self.per + n)


def every(ap, n):
    return ap.unsqueeze(1).to_broadcast([ap.shape[0], n, ap.shape[1]])


def each(ap, n):
    return ap.unsqueeze(2).to_broadcast([ap.shape[0], ap.shape[1], n])


def build(nc, I, out):
    ctx = ExitStack()
    with ctx:
        sb = lambda name, shape, dt=FP32: ctx.enter_context(nc.sbuf_tensor(name, shape, dt))
        sig = lambda name: Signal(ctx.enter_context(nc.semaphore(name)))
        dram = lambda name, shape: nc.dram_tensor(name, shape, FP32).ap()

        X = sb("X", [P, BLOCKS * DIM])
        H = sb("H", [P, BLOCKS * DIM])
        T1 = sb("T1", [P, BLOCKS * (WIDE + HEADS)])
        T2 = sb("T2", [P, BLOCKS * WIDE])
        W = sb("W", [P, 10 * DIM])
        iota = sb("iota", [P, P])
        ident = sb("ident", [P, P])
        ones = sb("ones", [P, P])
        lower = sb("lower", [P, P])
        pcol = sb("pcol", [P, 1])
        dloc = sb("dloc", [P, ALL])
        dend = sb("dend", [P, ALL])
        ew = sb("ew", [P, ALL])
        srci = sb("srci", [P, ALL], I32)
        brow = sb("brow", [1, ALL], I32)
        trow = sb("trow", [1, ALL], I32)
        LG = sb("LG", [P, HEADS * ALL])
        srcf = LG[:, 3 * ALL:4 * ALL]
        sidx = LG[:, 2 * ALL:2 * ALL + STEPS].bitcast(I32)
        cnt = sb("cnt", [P, BLOCKS])
        slot_idx = sb("slot_idx", [P, TURN], I32)
        goes_on = sb("goes_on", [HEADS, ALL])
        came_on = sb("came_on", [HEADS, ALL])
        pa_col = sb("pa_col", [P, 1])
        has = sb("has", [P, BLOCKS])
        slot_idx2 = sb("slot_idx2", [P, TURN], I32)
        small = sb("small", [P, 64])
        PS = ctx.enter_context(nc.psum_tensor("PS", [P, 4096], FP32))
        bank = lambda n, w=512: PS[:, 512 * n:512 * n + w]

        onehot_t_d = dram("onehot_t_d", [P, STEPS * P])
        packed_d = dram("packed_d", [ALL, 6 * P])
        step_src_d = dram("step_src_d", [ALL, P])
        step_dst_d = dram("step_dst_d", [ALL + 2, P])
        step_first_d = dram("step_first_d", [ALL, P])
        step_last_d = dram("step_last_d", [ALL, P])
        score_d = dram("score_d", [ROWS, 1])
        gather_d = dram("gather_d", [ROWS, DIM])
        wide_d = dram("wide_d", [ROWS, WIDE])
        edge_rows_d = dram("edge_rows_d", [P, STEPS * WIDE])
        ends_d = dram("ends_d", [HEADS, ALL + 2])
        ends2_d = dram("ends2_d", [HEADS, ALL + 2])
        added_d = [dram(f"added_{k}_d", [ROWS + P, DIM]) for k in range(COPIES)]

        vch, ach, gch = Chain(sig("vector_done")), Chain(sig("scalar_done")), Chain(sig("gpsimd_done"))
        loaded, stored = sig("loaded"), sig("stored")
        pe_done, ev_done, vv_done = sig("products_done"), sig("evicted"), sig("vector_ready")
        pe2_done, ac_done, v2_done = sig("products2_done"), sig("scalar_ready"), sig("vector2_ready")
        two = lambda name: [sig(f"{name}_{g}") for g in range(2)]
        rows_here, rows_free = two("rows_here"), two("rows_free")
        odd_rows_here, odd_saved = two("odd_rows_here"), two("odd_saved")
        tiles_here, tiles_free = two("tiles_here"), two("tiles_free")
        extra_here, extra_free = two("extra_here"), two("extra_free")
        saved = two("saved")
        pool_gate, scalar_gate = sig("pool_gate"), sig("scalar_gate")
        pA, pB, pC, pD, pE = (two(f"product_{k}") for k in "abcde")
        vA, vB, vC, vD = (two(f"vector_{k}") for k in "abcd")
        aA, aB = (two(f"scalar_{k}") for k in "ab")
        one_hots = two("one_hots")
        scattered = [sig(f"scattered_{k}") for k in range(COPIES)]
        scattered_read = [sig(f"scattered_read_{k}") for k in range(COPIES)]
        gch_done = sig("reduced")
        V, S_, T_, G = nc.vector, nc.scalar, nc.tensor, nc.gpsimd

        def blocks(tab, width):
            return tab[:, 0:BLOCKS * width].rearrange("p (t w) -> p t w", w=width)

        def numbers_of(eng, row, j, limit):
            _, values = nc.values_load_multi_w_load_instructions(
                row[0:1, bass.ds(j * TURN, TURN)], engines=(eng.engine,), min_val=0, max_val=limit - 1,
                skip_runtime_bounds_check_because="the row holds numbers below the limit alone")
            return values

        def blocks_of(eng, j):
            return numbers_of(eng, brow, j, BLOCKS)

        def setup():
            raw = T2[:, 0:4 * CHUNKS * P].bitcast(I32).rearrange("p (k c e) -> p k c e", k=4, e=P)
            pk = T1[:, 0:6 * ALL].rearrange("p (c k e) -> p c k e", k=6, e=P)
            cmp = H[:, 0:CHUNKS * ALL].rearrange("p (c s) -> p c s", c=CHUNKS)
            far = LG[:, 0:ALL].rearrange("p (c e) -> p c e", e=P)
            ewr = LG[:, ALL:2 * ALL].rearrange("p (c e) -> p c e", e=P)
            iota_s = LG[:, 2 * ALL:3 * ALL]
            trep = LG[:, 3 * ALL:4 * ALL]
            stepr = T2[:, 4 * ALL:10 * ALL].rearrange("p (c k e) -> p c k e", k=6, e=P)
            key, tcol, bcol = small[:, 0:7], small[:, 8:15], small[:, 16:23]
            keyi, tcoli = small[:, 24:31].bitcast(I32), small[:, 32:39].bitcast(I32)
            scol = small[:, 40:47]
            cview = lambda flat, off: flat[off:off + ALL * P].rearrange("(c p e) -> p c e", p=P, e=P)
            with nc.Block() as block:
                @block.sync
                def _(sp):
                    for k, off in ((1, 1), (2, 0), (3, 2)):
                        sp.dma_start(raw[:, k], cview(I["dst"], off)).then_inc(loaded.h, 16)
                    sp.dma_start(raw[:, 0], cview(I["src"], 0)).then_inc(loaded.h, 16)
                    sp.dma_start(ewr, cview(I["ew"], 0)).then_inc(loaded.h, 16)
                    sp.dma_start(blocks(X, DIM), I["x"].rearrange("(t p) f -> p t f", p=P)).then_inc(loaded.h, 16)
                    sp.wait_ge(vv_done.h, 2)
                    sp.dma_start(packed_d.rearrange("(c p) w -> p c w", p=P),
                                 pk.rearrange("p c k e -> p c (k e)")).then_inc(stored.h, 16)
                    sp.wait_ge(vv_done.h, 5)
                    mid = step_dst_d[1:ALL + 1, :]
                    for k, d in ((0, step_src_d), (1, mid), (3, step_first_d), (4, step_last_d)):
                        sp.dma_start(d.rearrange("(c p) e -> p c e", p=P), stepr[:, :, k, :]).then_inc(stored.h, 16)
                    sp.dma_start(step_dst_d[0:1, :], W[0:1, 0:P]).then_inc(stored.h, 16)
                    sp.dma_start(step_dst_d[ALL + 1:ALL + 2, :], W[0:1, 0:P]).then_inc(stored.h, 16)
                    sp.wait_ge(stored.h, 16 * 7)
                    sp.wait_ge(loaded.h, 16 * 6)

                @block.gpsimd
                def _(gp):
                    c = gch.on(gp)
                    gp.iota(iota[:, :], pattern=[[1, P]], base=0, channel_multiplier=0, allow_small_or_imprecise_dtypes=True)
                    gp.iota(iota_s, pattern=[[1, ALL]], base=0, channel_multiplier=0, allow_small_or_imprecise_dtypes=True)
                    gp.iota(pcol[:, :], pattern=[[1, 1]], base=0, channel_multiplier=1, allow_small_or_imprecise_dtypes=True)
                    gp.iota(scol, pattern=[[P, CHUNKS]], base=0, channel_multiplier=1, allow_small_or_imprecise_dtypes=True)
                    gp.memset(W[0:1, 0:P], -FAR)
                    gp.memset(ones[:, :], 1.0)
                    gp.memset(lower[:, :], 1.0)
                    c.link(gp.memset(ident[:, :], 0.0))
                    gp.affine_select(out=lower[:, :], in_=lower[:, :], compare_op=ALU.is_gt, fill=0.0,
                                     base=0, pattern=[[-1, P]], channel_multiplier=1)
                    gp.affine_select(out=ident[:, :], in_=ident[:, :], compare_op=ALU.not_equal, fill=1.0,
                                     base=0, pattern=[[-1, P]], channel_multiplier=1).then_inc(ac_done.h, 1)
                    gp.wait_ge(vv_done.h, 4)
                    gp.sem_inc(pool_gate.h, 1)
                    gp.wait_ge(stored.h, 16)
                    for k in range(CHUNKS):
                        gp.indirect_dma_start(stepr[:, k].rearrange("p k e -> p (k e)"), None, packed_d[:, :],
                                              bass.IndirectOffsetOnAxis(ap=tcoli[:, k:k + 1], axis=0)).then_inc(rows_here[0].h, 16)

                @block.vector
                def _(dve):
                    c = vch.on(dve)
                    dve.wait_ge(loaded.h, 16 * 6)
                    dve.wait_ge(ac_done.h, 1)
                    V.tensor_copy(pk[:, :, 0], raw[:, 0])
                    V.tensor_copy(pk[:, :, 5], ewr)
                    V.tensor_single_scalar(keyi, raw[:, 1, :, 0], 7, ALU.arith_shift_right)
                    V.tensor_tensor(pk[:, :, 3], raw[:, 1], raw[:, 2], ALU.not_equal)
                    V.tensor_tensor(pk[:, :, 4], raw[:, 1], raw[:, 3], ALU.not_equal)
                    V.tensor_copy(pk[:, :, 1], raw[:, 1])
                    c.link(V.tensor_scalar(far, raw[:, 1], FAR, None, ALU.add))
                    V.scalar_tensor_tensor(key, keyi, float(LEAD), scol, ALU.add, ALU.add)
                    c.link(V.tensor_tensor(far, far, pk[:, :, 4], ALU.mult))
                    V.tensor_scalar(pk[:, :, 2], far, -FAR, None, ALU.add)
                    V.tensor_scalar(pk[:, :, 3], pk[:, :, 3], -BIG, None, ALU.mult)
                    V.tensor_scalar(pk[:, :, 4], pk[:, :, 4], -BIG, None, ALU.mult).then_inc(vv_done.h, 2)
                    for k in range(CHUNKS):
                        last = V.tensor_scalar(cmp[:, k], iota_s, key[:, k:k + 1], None, ALU.is_ge)
                    last.then_inc(vv_done.h, 1)
                    dve.wait_ge(pe_done.h, 1)
                    half = ALL // 2
                    for h in range(2):
                        last = V.tensor_scalar(trep[:, h * half:(h + 1) * half], bank(h, half), -1.0, 0.0, ALU.add, ALU.max)
                    last.then_inc(v2_done.h, 1)
                    dve.wait_ge(v2_done.h, 1)
                    V.tensor_copy(trow[:, :], trep[0:1, :])
                    c.link(V.tensor_tensor(ewr.rearrange("p c e -> p (c e)"), iota_s, trep, ALU.subtract))
                    c.link(V.tensor_scalar(LG[0:1, ALL:2 * ALL], LG[0:1, ALL:2 * ALL], -float(LEAD), float(BLOCKS - 1), ALU.add, ALU.min))
                    V.tensor_scalar(brow[:, :], LG[0:1, ALL:2 * ALL], 0.0, None, ALU.max)
                    dve.wait_ge(pe_done.h, 2)
                    tr = PS[:, 1024:1024 + CHUNKS * P].rearrange("p (c e) -> p c e", e=P)[:, :, 0]
                    c.link(V.tensor_copy(tcol, tr))
                    V.tensor_copy(tcoli, tcol).then_inc(vv_done.h, 1)
                    c.link(V.tensor_tensor(bcol, scol, tcol, ALU.subtract))
                    c.link(V.tensor_scalar(bcol, bcol, float(P), -float(P * LEAD), ALU.mult, ALU.add))
                    dve.wait_ge(rows_here[0].h, 16 * CHUNKS)
                    for k in range(CHUNKS):
                        V.tensor_scalar(far[:, k], stepr[:, k, 1], bcol[:, k:k + 1], None, ALU.subtract)
                        last = V.tensor_scalar(stepr[:, k, 2], stepr[:, k, 2], bcol[:, k:k + 1], None, ALU.subtract)
                    last.then_inc(vv_done.h, 1)
                    for n, dst in enumerate((dloc, dend, ew, srci)):
                        dve.wait_ge(pe2_done.h, n + 1)
                        if n == 3:
                            V.tensor_copy(srcf[:, :], PS[:, 1024 * (n % 2):1024 * (n % 2) + ALL])
                        V.tensor_copy(dst[:, :], PS[:, 1024 * (n % 2):1024 * (n % 2) + ALL]).then_inc(v2_done.h, 1)
                    dve.wait_ge(v2_done.h, 5)

                @block.tensor
                def _(pe):
                    pe.wait_ge(ac_done.h, 1)
                    pe.wait_ge(vv_done.h, 3)
                    half = ALL // 2
                    for h in range(2):
                        for k in range(CHUNKS):
                            last = T_.matmul(bank(h, half), ones[:, :], cmp[:, k, h * half:(h + 1) * half],
                                             start=k == 0, stop=k == CHUNKS - 1)
                    last.then_inc(pe_done.h, 1)
                    pe.wait_ge(v2_done.h, 1)
                    for k in range(CHUNKS):
                        last = T_.transpose(PS[:, 1024 + k * P:1024 + (k + 1) * P], trep[:, k * P:(k + 1) * P], ident[:, :])
                    last.then_inc(pe_done.h, 1)
                    pe.wait_ge(vv_done.h, 5)
                    for n in range(4):
                        pe.wait_ge(v2_done.h, max(1, n))
                        for k in range(CHUNKS):
                            src = (far[:, k], stepr[:, k, 2], stepr[:, k, 5], stepr[:, k, 0])[n]
                            o = 1024 * (n % 2) + k * P
                            last = T_.transpose(PS[:, o:o + P], src, ident[:, :])
                        last.then_inc(pe2_done.h, 1)
            for s, n in ((loaded, 96), (stored, 112), (vv_done, 5), (ac_done, 1), (pe_done, 2), (pe2_done, 4),
                         (v2_done, 5), (rows_here[0], 16 * CHUNKS), (pool_gate, 1)):
                s.passed(n)

        def layernorm():
            x3, h3 = blocks(X, DIM), blocks(H, DIM)
            q3 = blocks(T2, DIM)
            m, v = small[:, 0:BLOCKS], LG[:, 0:BLOCKS]
            with nc.Block() as block:
                @block.vector
                def _(dve):
                    c = vch.on(dve)
                    c.link(V.tensor_reduce(m, x3, AX.X, ALU.add))
                    c.link(V.tensor_scalar(m, m, 1.0 / DIM, None, ALU.mult))
                    c.link(V.tensor_tensor(h3, x3, each(m, DIM), ALU.subtract))
                    c.link(V.tensor_tensor(q3, h3, h3, ALU.mult))
                    c.link(V.tensor_reduce(v, q3, AX.X, ALU.add))
                    V.tensor_scalar(v, v, 1.0 / DIM, 1e-5, ALU.mult, ALU.add).then_inc(vv_done.h, 1)
                    dve.wait_ge(ac_done.h, ac_done.at(1))
                    c.link(V.reciprocal(v, v))
                    V.tensor_tensor(h3, h3, each(v, DIM), ALU.mult).then_inc(vv_done.h, 1)

                @block.scalar
                def _(act):
                    act.wait_ge(vv_done.h, vv_done.at(1))
                    S_.activation(v, v, ACT.Sqrt).then_inc(ac_done.h, 1)
                    act.wait_ge(vv_done.h, vv_done.at(2))
                    S_.activation(H[:, :], H[:, :], ACT.Relu).then_inc(ac_done.h, 1)
            vv_done.passed(2)
            ac_done.passed(2)

        def load_weights(items):
            with nc.Block() as block:
                @block.sync
                def _(sp):
                    for at, parts, ap, *first in items:
                        p0 = first[0] if first else 0
                        sp.dma_start(W[p0:p0 + parts, at:at + ap.shape[1]], ap).then_inc(loaded.h, 16)
                    sp.wait_ge(loaded.h, loaded.at(16 * len(items)))
            loaded.passed(16 * len(items))

        wcol = lambda k, parts=P: W[0:parts, k * DIM:(k + 1) * DIM]
        bias_row = lambda ap, n=DIM: ap.rearrange("(a n) -> a n", a=1)[0:1, 0:n].to_broadcast([P, n])

        def node_linear(srcs, outs, stage):
            K = len(srcs)
            view = lambda spec, j: (spec[0][:, bass.ds(j * (NB * spec[1]), NB * spec[1])]
                                    .rearrange("p (u w) -> p u w", w=spec[1])[:, :, spec[2]:spec[2] + DIM])
            room = [stage[:, k * NB * DIM:(k + 1) * NB * DIM] for k in range(2 * K)]
            n_out = len(outs)
            with nc.Block() as block:
                @block.scalar
                def _(act):
                    with act.Fori(0, BLOCKS // NB) as j:
                        act.wait_ge(pB[0].h, pB[0].at(j * n_out + 1))
                        for k in range(K):
                            S_.activation(room[k].rearrange("p (u w) -> p u w", w=DIM), view(srcs[k], j),
                                          ACT.Copy).then_inc(aA[0].h, 1)
                        for k in range(K):
                            act.wait_ge(pA[0].h, pA[0].at(j * K + k + 1))
                            S_.activation(room[K + k], PS[:, 1024 * (k % 2):1024 * (k % 2) + NB * DIM], ACT.Copy).then_inc(aB[0].h, 1)

                @block.tensor
                def _(pe):
                    pe.sem_inc(pB[0].h, 1)
                    with pe.Fori(0, BLOCKS // NB) as j:
                        for k in range(K):
                            pe.wait_ge(aA[0].h, aA[0].at(j * K + k + 1))
                            if k >= 2:
                                pe.wait_ge(aB[0].h, aB[0].at(j * K + k - 1))
                            for u in range(NB):
                                o = 1024 * (k % 2) + u * P
                                last = T_.transpose(PS[:, o:o + P], room[k][:, u * P:(u + 1) * P], ident[:, :])
                            last.then_inc(pA[0].h, 1)
                        pe.wait_ge(aB[0].h, aB[0].at(j * K + K))
                        for n, o in enumerate(outs):
                            pe.wait_ge(v2_done.h, v2_done.at(j * n_out + n + (2 if n == 0 and n_out % 2 else 1)))
                            for u in range(NB):
                                at = 2048 + 1024 * (n % 2) + u * P
                                for k in range(K):
                                    last = T_.matmul(PS[:, at:at + P], room[K + k][:, u * P:(u + 1) * P], o["w"][k],
                                                     start=k == 0, stop=k == K - 1)
                            last.then_inc(pB[0].h, 1)

                @block.vector
                def _(dve):
                    c = vch.on(dve)
                    dve.sem_inc(v2_done.h, 2)
                    with dve.Fori(0, BLOCKS // NB) as j:
                        c.open(j, sum((o.get("plus") is not None) + bool(o.get("relu")) for o in outs))
                        for n, o in enumerate(outs):
                            at = 2048 + 1024 * (n % 2)
                            src = PS[:, at:at + NB * DIM].rearrange("p (u w) -> p u w", w=DIM)
                            to = view(o["to"], j)
                            dve.wait_ge(pB[0].h, pB[0].at(j * n_out + n + 2))
                            if o.get("plus") is not None:
                                c.link(V.tensor_tensor(to, src, view(o["plus"], j), ALU.add))
                                src = to
                            last = V.tensor_tensor(to, src, every(o["add"], NB), ALU.add)
                            if o.get("relu"):
                                c.link(last)
                                last = V.tensor_scalar(to, to, 0.0, None, ALU.max)
                            last.then_inc(v2_done.h, 1)
                    c.close(BLOCKS // NB)
            trips = BLOCKS // NB
            for s, n in ((v2_done, trips * n_out + 2), (aA[0], trips * K), (aB[0], trips * K),
                         (pA[0], trips * K), (pB[0], trips * n_out + 1)):
                s.passed(n)

        def edge_weights():
            w = LG[:, 0:STEPS]
            dup = LG[:, ALL:ALL + STEPS]
            tcols = LG[:, 2 * ALL:2 * ALL + BLOCKS]
            at = 0

            def room(n):
                nonlocal at
                at += n
                return T2[:, at - n:at]
            O8, OT8, SR8, EQ8 = (room(2 * GROUP * P) for _ in range(4))
            sg = room(TURN)
            G4 = GROUP * P
            tables = room(3 * BLOCKS)
            counts = [cnt] + [tables[:, k * BLOCKS:(k + 1) * BLOCKS] for k in range(3)]

            def one_hots_of(g, first):
                O4 = O8[:, g * G4:(g + 1) * G4].rearrange("p (u e) -> p u e", e=P)
                V.tensor_tensor(O4, every(iota[:, :], 4), each(dloc[:, bass.ds(first + 4 * g, 4)], P), ALU.is_equal).then_inc(one_hots[g].h, 1)

            def take_scores(dve, j, g):
                dve.wait_ge(rows_here[g].h, rows_here[g].at(64 * j + 64))
                V.tensor_copy(w[:, bass.ds(j * TURN + 4 * g, 4)], sg[:, 4 * g:4 * g + 4]).then_inc(rows_free[g].h, 1)

            with nc.Block() as block:
                @block.gpsimd
                def _(gp):
                    c = gch.on(gp)
                    with gp.Fori(0, TURNS + 1) as j:
                        c.open(j, 2)
                        for g in range(2):
                            gp.wait_ge(rows_free[g].h, rows_free[g].at(j + 1))
                            c.link(G.tensor_copy(slot_idx[:, 4 * g:4 * g + 4], srci[:, bass.ds(j * TURN + 4 * g, 4)]))
                            gp.sem_inc(pool_gate.h, 1)
                            for u in range(4):
                                k = 4 * g + u
                                gp.indirect_dma_start(sg[:, k:k + 1], None, score_d[:, :], bass.IndirectOffsetOnAxis(
                                    ap=slot_idx[:, k:k + 1], axis=0)).then_inc(rows_here[g].h, 16)
                    c.close(TURNS + 1)

                @block.sync
                def _(sp):
                    with sp.Fori(0, TURNS + 1) as j:
                        for g in range(2):
                            sp.wait_ge(tiles_free[g].h, tiles_free[g].at(j + 1))
                            row = step_src_d[bass.ds(j * TURN + 4 * g, 4), :].rearrange("(a s) e -> a (s e)", a=1)
                            sp.dma_start(SR8[:, g * G4:(g + 1) * G4], row.to_broadcast([P, G4])).then_inc(tiles_here[g].h, 16)
                        for g in range(2):
                            sp.wait_ge(aA[g].h, aA[g].at(j + 1))
                            sp.dma_start(onehot_t_d[:, bass.ds(j * TURN * P + g * G4, G4)],
                                         OT8[:, g * G4:(g + 1) * G4]).then_inc(saved[g].h, 16)
                        for g in range(2):
                            sp.wait_ge(saved[g].h, saved[g].at(16 * j + 16))
                            sp.sem_inc(extra_free[g].h, 1)

                @block.tensor
                def _(pe):
                    with pe.Fori(0, TURNS + 1) as j:
                        bs = blocks_of(pe, j)
                        for g in range(2):
                            pe.wait_ge(one_hots[g].h, one_hots[g].at(j + 1))
                            for u in range(4):
                                o = g * G4 + u * P
                                last = T_.transpose(bank(g)[:, u * P:(u + 1) * P], O8[:, o:o + P], ident[:, :])
                            last.then_inc(pA[g].h, 1)
                        for g in range(2):
                            pe.wait_ge(aA[g].h, aA[g].at(j + 1))
                            pe.wait_ge(vA[g].h, vA[g].at(j + 1))
                            for u in range(4):
                                o = g * G4 + u * P
                                T_.matmul(bank(2 + g)[:, u:u + 1], OT8[:, o:o + P], tcols[:, bass.ds(bs[4 * g + u], 1)], start=True, stop=True)
                                last = T_.matmul(bank(2 + g)[:, 8 + u:9 + u], O8[:, o:o + P], ones[:, 0:1], start=True, stop=True)
                            last.then_inc(pB[g].h, 1)

                @block.scalar
                def _(act):
                    with act.Fori(0, TURNS + 1) as j:
                        for g in range(2):
                            act.wait_ge(pA[g].h, pA[g].at(j + 1))
                            act.wait_ge(extra_free[g].h, extra_free[g].at(j + 1))
                            act.wait_ge(vA[g].h, vA[g].at(j + 1))
                            S_.activation(OT8[:, g * G4:(g + 1) * G4], bank(g), ACT.Copy).then_inc(aA[g].h, 1)

                @block.vector
                def _(dve):
                    c = vch.on(dve)
                    V.memset(cnt[:, :], 0.0)
                    c.link(V.memset(tables, 0.0))
                    for g in range(2):
                        dve.sem_inc(rows_free[g].h, 1)
                        dve.sem_inc(tiles_free[g].h, 1)
                        dve.sem_inc(vA[g].h, 1)
                        dve.sem_inc(extra_free[g].h, 1)
                        one_hots_of(g, 0)
                    with dve.Fori(0, TURNS + 1) as j:
                        c.open(j, 4)
                        bs = blocks_of(dve, j)
                        for g in range(2):
                            s0 = j * TURN + 4 * g
                            EQ = EQ8[:, g * G4:(g + 1) * G4].rearrange("p (u e) -> p u e", e=P)
                            SR = SR8[:, g * G4:(g + 1) * G4].rearrange("p (u e) -> p u e", e=P)
                            dve.wait_ge(tiles_here[g].h, tiles_here[g].at(16 * j + 16))
                            c.link(V.tensor_tensor(EQ, SR, each(srcf[:, bass.ds(s0, 4)], P), ALU.is_equal))
                            c.link(V.tensor_tensor(EQ, EQ, every(lower[:, :], 4), ALU.mult))
                            V.tensor_reduce(dup[:, bass.ds(s0, 4)], EQ, AX.X, ALU.add).then_inc(tiles_free[g].h, 1)
                            if g == 0:
                                take_scores(dve, j, 0)
                        for g in range(2):
                            if g == 1:
                                take_scores(dve, j, 1)
                            wg = w[:, bass.ds(j * TURN + 4 * g, 4)]
                            dve.wait_ge(pB[g].h, pB[g].at(j + 1))
                            dve.wait_ge(rows_free[g].h, rows_free[g].at(j + 2))
                            V.tensor_tensor(wg, wg, bank(2 + g)[:, 0:4], ALU.add)
                            for u in range(4):
                                o = counts[u][:, bass.ds(bs[4 * g + u], 1)]
                                last = V.tensor_tensor(o, o, bank(2 + g)[:, 8 + u:9 + u], ALU.add)
                            last.then_inc(vB[0].h, 1)
                            dve.wait_ge(vB[0].h, vB[0].at(j * 2 + (g + 1)))
                            dve.sem_inc(vA[g].h, 1)
                            one_hots_of(g, (j + 1) * TURN)
                    c.close(TURNS + 1)
                    for u in range(1, 4):
                        c.link(V.tensor_tensor(cnt[:, :], cnt[:, :], counts[u], ALU.add))
            turns = TURNS + 1
            for g in range(2):
                for s, n in ((rows_free[g], turns + 1), (tiles_free[g], turns + 1), (vA[g], turns + 1),
                             (extra_free[g], turns + 1), (saved[g], 16 * turns), (rows_here[g], 64 * turns), (tiles_here[g], 16 * turns),
                             (aA[g], turns), (pA[g], turns), (pB[g], turns), (one_hots[g], turns + 1)):
                    s.passed(n)
            vB[0].passed(2 * turns)
            pool_gate.passed(2 * turns)

        def softmax_over_edges():
            w, dup, t = LG[:, 0:STEPS], LG[:, ALL:ALL + STEPS], T2[:, 0:STEPS]
            mx, ax, sm, asm_ = (small[:, k:k + 1] for k in range(4))
            with nc.Block() as block:
                @block.vector
                def _(dve):
                    c = vch.on(dve)
                    d = dloc[:, 0:STEPS]
                    c.link(V.tensor_scalar(t, d, 0.0, None, ALU.is_ge))
                    c.link(V.scalar_tensor_tensor(t, d, float(P), t, ALU.is_lt, ALU.mult))
                    c.link(V.scalar_tensor_tensor(w, w, 0.01, w, ALU.mult, ALU.max))
                    c.link(V.tensor_tensor(w, w, t, ALU.mult))
                    c.link(V.tensor_scalar(t, t, BIG, -BIG, ALU.mult, ALU.add))
                    c.link(V.tensor_tensor(w, w, t, ALU.add))
                    V.tensor_reduce(mx, w, AX.X, ALU.max).then_inc(vv_done.h, 1)
                    c.link(V.tensor_scalar(dup, dup, 1.0, None, ALU.min))
                    tr = small[:, 8:9]
                    c.link(V.tensor_scalar(tr, pcol[:, :], float(TRASH), None, ALU.add))
                    q = T2[:, ALL:ALL + STEPS]
                    c.link(V.tensor_scalar(q, srcf[:, 0:STEPS], -1.0, tr, ALU.mult, ALU.add))
                    c.link(V.tensor_tensor(q, q, dup, ALU.mult))
                    c.link(V.tensor_tensor(sidx, q, srcf[:, 0:STEPS], ALU.add))
                    dve.wait_ge(gch_done.h, gch_done.at(1))
                    V.tensor_scalar(ax, ax, -1.0, None, ALU.mult).then_inc(vv_done.h, 1)
                    dve.wait_ge(gch_done.h, gch_done.at(2))
                    c.link(V.reciprocal(asm_, asm_))
                    c.link(V.tensor_scalar(w, w, asm_, None, ALU.mult))

                @block.gpsimd
                def _(gp):
                    gp.wait_ge(vv_done.h, vv_done.at(1))
                    G.partition_all_reduce(ax, mx, P, bass.bass_isa.ReduceOp.max).then_inc(gch_done.h, 1)
                    gp.wait_ge(ac_done.h, ac_done.at(1))
                    G.partition_all_reduce(asm_, sm, P, bass.bass_isa.ReduceOp.add).then_inc(gch_done.h, 1)

                @block.scalar
                def _(act):
                    act.wait_ge(vv_done.h, vv_done.at(2))
                    S_.activation(w, w, ACT.Exp, bias=ax, accum_out=sm).then_inc(ac_done.h, 1)
            for s, n in ((vv_done, 2), (gch_done, 2), (ac_done, 1)):
                s.passed(n)

        def add_messages():
            w = LG[:, 0:STEPS]
            OT8, SR8, EQ8, MS8, OUT8 = (T2[:, k * TURN * P:(k + 1) * TURN * P] for k in range(5))
            zeros = T2[:, 5 * TURN * P + 1024:5 * TURN * P + 1024 + ROWS + P]
            G4 = GROUP * P
            quad = lambda buf, g: buf[:, g * G4:(g + 1) * G4]
            with nc.Block() as block:
                @block.sync
                def _(sp):
                    with sp.Fori(0, TURNS) as j:
                        for g in range(2):
                            sp.wait_ge(pA[g].h, pA[g].last(j))
                            sp.dma_start(quad(OT8, g), onehot_t_d[:, bass.ds(j * TURN * P + g * G4, G4)]).then_inc(tiles_here[g].h, 16)
                            sp.wait_ge(vA[g].h, vA[g].last(j))
                            row = step_src_d[bass.ds(j * TURN + 4 * g, 4), :].rearrange("(a s) e -> a (s e)", a=1)
                            sp.dma_start(quad(SR8, g), row.to_broadcast([P, G4])).then_inc(tiles_here[g].h, 16)

                @block.tensor
                def _(pe):
                    for g in range(2):
                        pA[g].start(pe)
                        pB[g].start(pe)
                    with pe.Fori(0, TURNS) as j:
                        bs = blocks_of(pe, j)
                        for g in range(2):
                            pe.wait_ge(tiles_here[g].h, tiles_here[g].at(32 * j + 32))
                            pe.wait_ge(vA[g].h, vA[g].last(j))
                            for u in range(4):
                                last = T_.matmul(bank(g)[:, u * P:(u + 1) * P], quad(OT8, g)[:, u * P:(u + 1) * P],
                                                 T1[:, bass.ds(bs[4 * g + u] * DIM, DIM)], start=True, stop=True)
                            last.then_inc(pA[g].h, 1)
                        for g in range(2):
                            pe.wait_ge(vA[g].h, vA[g].turn(j))
                            pe.wait_ge(aA[g].h, aA[g].last(j))
                            for u in range(4):
                                last = T_.matmul(bank(2 + g)[:, u * P:(u + 1) * P], quad(EQ8, g)[:, u * P:(u + 1) * P],
                                                 quad(MS8, g)[:, u * P:(u + 1) * P], start=True, stop=True)
                            last.then_inc(pB[g].h, 1)

                @block.vector
                def _(dve):
                    V.memset(zeros, 0.0).then_inc(vv_done.h, 1)
                    for g in range(2):
                        vA[g].start(dve)
                    with dve.Fori(0, TURNS) as j:
                        for g in range(2):
                            s0 = j * TURN + 4 * g
                            split = lambda buf: quad(buf, g).rearrange("p (u e) -> p u e", e=P)
                            dve.wait_ge(tiles_here[g].h, tiles_here[g].at(32 * j + 32))
                            dve.wait_ge(pB[g].h, pB[g].last(j))
                            V.tensor_tensor(split(EQ8), split(SR8), each(srcf[:, bass.ds(s0, 4)], P), ALU.is_equal)
                            dve.wait_ge(pA[g].h, pA[g].turn(j))
                            V.tensor_tensor(split(MS8), bank(g).rearrange("p (u e) -> p u e", e=P),
                                            each(w[:, bass.ds(s0, 4)], P), ALU.mult).then_inc(vA[g].h, 1)

                @block.scalar
                def _(act):
                    for g in range(2):
                        aA[g].start(act)
                    with act.Fori(0, TURNS) as j:
                        for g in range(2):
                            act.wait_ge(pB[g].h, pB[g].turn(j))
                            for u in range(4):
                                act.wait_ge(scattered[4 * g + u].h, scattered[4 * g + u].at(16 * j + 16))
                            S_.activation(quad(OUT8, g), bank(2 + g), ACT.Copy).then_inc(aA[g].h, 1)

                @block.gpsimd
                def _(gp):
                    c = gch.on(gp)
                    gp.wait_ge(vv_done.h, vv_done.at(1))
                    for k in range(COPIES):
                        gp.dma_start(added_d[k].rearrange("(t p) f -> p t f", p=P),
                                     zeros.rearrange("p (t f) -> p t f", f=DIM)).then_inc(scattered[k].h, 16)
                    with gp.Fori(0, TURNS) as j:
                        c.open(j, 2)
                        for g in range(2):
                            gp.wait_ge(aA[g].h, aA[g].turn(j))
                            c.link(G.tensor_copy(slot_idx[:, 4 * g:4 * g + 4], sidx[:, bass.ds(j * TURN + 4 * g, 4)]))
                            gp.sem_inc(pool_gate.h, 1)
                            for u in range(4):
                                k = 4 * g + u
                                gp.indirect_dma_start(added_d[k][:, :], bass.IndirectOffsetOnAxis(ap=slot_idx[:, k:k + 1], axis=0),
                                                      quad(OUT8, g)[:, u * P:(u + 1) * P], None,
                                                      compute_op=ALU.add).then_inc(scattered[k].h, 16)
                    c.close(TURNS)
                    for k in range(COPIES):
                        gp.wait_ge(scattered[k].h, scattered[k].at(16 * TURNS + 16))
            for g in range(2):
                for s, n in ((pA[g], TURNS + 1), (pB[g], TURNS + 1), (vA[g], TURNS + 1), (aA[g], TURNS + 1),
                             (tiles_here[g], 32 * TURNS)):
                    s.passed(n)
            for k in range(COPIES):
                scattered[k].passed(16 * TURNS + 16)
            vv_done.passed(1)
            pool_gate.passed(2 * TURNS)

            halves = [T1[:, 0:ROWS], T1[:, ROWS:2 * ROWS], T2[:, 0:ROWS], T2[:, ROWS:2 * ROWS]]
            with nc.Block() as block:
                @block.sync
                def _(sp):
                    for k in range(COPIES):
                        if k >= 4:
                            sp.wait_ge(vv_done.h, vv_done.at(k - 3))
                        sp.dma_start(halves[k % 4].rearrange("p (t f) -> p t f", f=DIM),
                                     added_d[k][0:ROWS, :].rearrange("(t p) f -> p t f", p=P)).then_inc(scattered_read[k].h, 16)

                @block.vector
                def _(dve):
                    for k in range(COPIES):
                        dve.wait_ge(scattered_read[k].h, 16)
                        V.tensor_tensor(X[:, :], X[:, :], halves[k % 4], ALU.add).then_inc(vv_done.h, 1)
                        dve.wait_ge(vv_done.h, vv_done.at(k + 1))
            vv_done.passed(COPIES)

        def table_to_dram(tab, width, dst):
            with nc.Block() as block:
                @block.sync
                def _(sp):
                    sp.dma_start(dst.rearrange("(t p) f -> p t f", p=P), blocks(tab, width)).then_inc(stored.h, 16)
                    sp.wait_ge(stored.h, stored.at(16))
            stored.passed(16)

        def layer0():
            load_weights([(0, P, I["L0_W_w"]), (DIM, P, bias_row(I["L0_W_b"])),
                          (2 * DIM, P, bias_row(I["L0_a_w"])), (3 * DIM, P, bias_row(I["L0_a_w2"])),
                          (4 * DIM, P, bias_row(I["L0_a_b"], 1))])
            layernorm()
            node_linear([(H, DIM, 0)], [dict(w=[wcol(0)], add=wcol(1), to=(T1, DIM, 0))], T2)
            tab, q = blocks(T1, DIM), blocks(T2, DIM)
            sc, tc = small[:, 0:BLOCKS], LG[:, 2 * ALL:2 * ALL + BLOCKS]
            with nc.Block() as block:
                @block.vector
                def _(dve):
                    c = vch.on(dve)
                    c.link(V.tensor_tensor(q, tab, every(wcol(2), BLOCKS), ALU.mult))
                    c.link(V.tensor_reduce(sc, q, AX.X, ALU.add))
                    c.link(V.tensor_tensor(q, tab, every(wcol(3), BLOCKS), ALU.mult))
                    c.link(V.tensor_reduce(tc, q, AX.X, ALU.add))
                    V.tensor_scalar(tc, tc, W[:, 4 * DIM:4 * DIM + 1], None, ALU.add).then_inc(vv_done.h, 1)

                @block.sync
                def _(sp):
                    sp.wait_ge(vv_done.h, vv_done.at(1))
                    with nc.allow_non_contiguous_dma(reason="one score per node"):
                        sp.dma_start(score_d.rearrange("(t p) a -> p t a", p=P), sc.unsqueeze(2)).then_inc(stored.h, 16)
                    sp.wait_ge(stored.h, stored.at(16))
            vv_done.passed(1)
            stored.passed(16)
            edge_weights()
            softmax_over_edges()
            add_messages()

        def gather_rows(gp, table, rows, width, free, ahead=0):
            c = gch.on(gp)
            with gp.Fori(0, TURNS) as j:
                c.open(j, 2)
                for g in range(2):
                    free(g, j)
                    c.link(G.tensor_copy(slot_idx[:, 4 * g:4 * g + 4], srci[:, bass.ds((j + ahead) * TURN + 4 * g, 4)]))
                    gp.sem_inc(pool_gate.h, 1)
                    for u in range(4):
                        k = 4 * g + u
                        gp.indirect_dma_start(rows[:, k * width:(k + 1) * width], None, table[:, :],
                                              bass.IndirectOffsetOnAxis(ap=slot_idx[:, k:k + 1], axis=0)).then_inc(rows_here[g].h, 16)
            c.close(TURNS)

        def one_hot(buf, g, places, s0):
            return V.tensor_tensor(buf[:, g * GROUP * P:(g + 1) * GROUP * P].rearrange("p (u e) -> p u e", e=P),
                                   every(iota[:, :], 4), each(places[:, bass.ds(s0, 4)], P), ALU.is_equal)

        def add_to_table(c, tables, width, bs, products):
            for u in range(4):
                o = tables[u % len(tables)][:, bass.ds(bs[u] * width, width)]
                c.link(V.tensor_tensor(o, o, products[u], ALU.add), running=len(tables) - 1 if u < 3 else 0)

        quad = lambda buf, g, w=P: buf[:, g * GROUP * w:(g + 1) * GROUP * w]
        split = lambda ap, w=P: ap.rearrange("p (u e) -> p u e", e=w)
        part = lambda ap, u, w=P: ap[:, u * w:(u + 1) * w]

        def edge_mlp_sums():
            R8, O8, M8, EAT8, EA8 = (T2[:, k * TURN * P:(k + 1) * TURN * P] for k in range(5))
            with nc.Block() as block:
                @block.gpsimd
                def _(gp):
                    gather_rows(gp, gather_d, R8, DIM, lambda g, j: gp.wait_ge(vA[g].h, vA[g].last(j)))

                @block.sync
                def _(sp):
                    with sp.Fori(0, TURNS) as j:
                        ts = numbers_of(sp, trow, j, TILES)
                        for g in range(2):
                            sp.wait_ge(pA[g].h, pA[g].last(j))
                            for u in range(4):
                                sp.dma_start(part(quad(EA8, g, EDGE_DIM), u, EDGE_DIM),
                                             I["ea"][bass.ds(ts[4 * g + u] * P, P), :]).then_inc(tiles_here[g].h, 16)

                @block.tensor
                def _(pe):
                    for g in range(2):
                        for s in (pA, pB, pC):
                            s[g].start(pe)
                    with pe.Fori(0, TURNS) as j:
                        for g in range(2):
                            pe.wait_ge(tiles_here[g].h, tiles_here[g].at(64 * j + 64))
                            pe.wait_ge(aA[g].h, aA[g].last(j))
                            for v in range(2):
                                last = T_.transpose(part(bank(g), v), part(quad(EA8, g, EDGE_DIM), v), ident[:, :])
                            last.then_inc(pA[g].h, 1)
                        for g in range(2):
                            pe.wait_ge(aA[g].h, aA[g].turn(j))
                            pe.wait_ge(vA[g].h, vA[g].last(j))
                            for u in range(4):
                                half = slice(EDGE_DIM * (u % 2), EDGE_DIM * (u % 2 + 1))
                                last = T_.matmul(part(bank((2, 6)[u % 2] + g), u // 2), part(quad(EAT8, g, EDGE_DIM), u // 2)[half], wcol(2)[half], start=True, stop=True)
                            last.then_inc(pB[g].h, 1)
                        for g in range(2):
                            pe.wait_ge(aB[g].h, aB[g].turn(j))
                            pe.wait_ge(vB[g].h, vB[g].turn(j))
                            pe.wait_ge(vC[g].h, vC[g].last(j))
                            for u in range(4):
                                last = T_.matmul(part(bank(4 + g), u), part(quad(O8, g), u), part(quad(M8, g), u), start=True, stop=True)
                            last.then_inc(pC[g].h, 1)

                @block.scalar
                def _(act):
                    for g in range(2):
                        aA[g].start(act)
                        aB[g].start(act)
                    with act.Fori(0, TURNS) as j:
                        for g in range(2):
                            act.wait_ge(pA[g].h, pA[g].turn(j))
                            act.wait_ge(pB[g].h, pB[g].last(j))
                            S_.activation(quad(EAT8, g, EDGE_DIM), bank(g, 2 * P), ACT.Copy).then_inc(aA[g].h, 1)
                        for g in range(2):
                            act.wait_ge(vA[g].h, vA[g].turn(j))
                            S_.activation(quad(M8, g), quad(M8, g), ACT.Relu).then_inc(aB[g].h, 1)

                @block.vector
                def _(dve):
                    c = vch.on(dve)
                    c.link(V.memset(T1[:, 0:2 * ROWS], 0.0))
                    for g in range(2):
                        for s in (vA, vB, vC):
                            s[g].start(dve)
                    with dve.Fori(0, TURNS) as j:
                        c.open(j, 8)
                        bs = blocks_of(dve, j)
                        for g in range(2):
                            dve.wait_ge(pC[g].h, pC[g].last(j))
                            one_hot(O8, g, dloc, j * TURN + 4 * g).then_inc(vB[g].h, 1)
                        for g in range(2):
                            dve.wait_ge(rows_here[g].h, rows_here[g].at(64 * j + 64))
                            dve.wait_ge(pB[g].h, pB[g].turn(j))
                            for half in range(2):
                                pick = lambda buf: split(quad(buf, g))[:, half::2]
                                last = V.tensor_tensor(pick(M8), split(bank((2, 6)[half] + g, 2 * P)), pick(R8), ALU.add)
                            last.then_inc(vA[g].h, 1)
                        for g in range(2):
                            dve.wait_ge(pC[g].h, pC[g].turn(j))
                            add_to_table(c, (T1[:, 0:ROWS], T1[:, ROWS:2 * ROWS]), DIM, bs[4 * g:4 * g + 4], [part(bank(4 + g), u) for u in range(4)])
                            dve.sem_inc(vC[g].h, 1)
                    c.close(TURNS)
            for g in range(2):
                for s in (pA, pB, pC, aA, aB, vA, vB, vC):
                    s[g].passed(TURNS + 1)
                rows_here[g].passed(64 * TURNS)
                tiles_here[g].passed(64 * TURNS)
            pool_gate.passed(2 * TURNS)

        def clipped_counts(dve, c):
            c.link(V.tensor_scalar(small[:, 0:BLOCKS], cnt[:, :], 1.0, None, ALU.max))
            c.link(V.reciprocal(small[:, 0:BLOCKS], small[:, 0:BLOCKS]))
            c.link(V.tensor_scalar(has[:, :], cnt[:, :], 1.0, None, ALU.min))

        def layer1():
            layernorm()
            load_weights([(0, P, I["L1_W1a"][0:DIM, :]), (DIM, P, bias_row(I["L1_b1a"])),
                          (2 * DIM, EDGE_DIM, I["L1_W1a"][DIM:DIM + EDGE_DIM, :]),
                          (2 * DIM, EDGE_DIM, I["L1_W1a"][DIM:DIM + EDGE_DIM, :], EDGE_DIM)])
            node_linear([(H, DIM, 0)], [dict(w=[wcol(0)], add=wcol(1), to=(T1, DIM, 0))], T2)
            table_to_dram(T1, DIM, gather_d)
            edge_mlp_sums()
            w2 = I["L1_W2a"]
            load_weights([(0, P, I["L1_W1b"]), (DIM, P, bias_row(I["L1_b1b"])), (2 * DIM, P, w2[0:P, :]),
                          (3 * DIM, P, w2[P:2 * P, :]), (4 * DIM, EDGE_DIM, w2[2 * P:2 * P + EDGE_DIM, :]),
                          (5 * DIM, P, bias_row(I["L1_b2a"])), (6 * DIM, P, I["L1_W2b"]),
                          (7 * DIM, P, bias_row(I["L1_b2b"])),
                          (8 * DIM, EDGE_DIM, I["L1_u"][0:1, :].rearrange("a n -> n a"))])
            sums = blocks(T1, DIM)
            with nc.Block() as block:
                @block.vector
                def _(dve):
                    c = vch.on(dve)
                    clipped_counts(dve, c)
                    c.link(V.tensor_tensor(T1[:, 0:ROWS], T1[:, 0:ROWS], T1[:, ROWS:2 * ROWS], ALU.add))
                    c.link(V.tensor_tensor(sums, sums, each(small[:, 0:BLOCKS], DIM), ALU.mult))
                    c.link(V.tensor_copy(W[0:EDGE_DIM, 9 * DIM:10 * DIM], W[0:EDGE_DIM, 8 * DIM:8 * DIM + 1].to_broadcast([EDGE_DIM, DIM])))
                    dve.sem_inc(vv_done.h, 1)
                    dve.wait_ge(pe_done.h, pe_done.at(1))
                    c.link(V.tensor_tensor(wcol(5), wcol(5), bank(0, DIM), ALU.add))

                @block.tensor
                def _(pe):
                    pe.wait_ge(vv_done.h, vv_done.at(1))
                    T_.matmul(bank(0, DIM), W[0:EDGE_DIM, 9 * DIM:10 * DIM], W[0:EDGE_DIM, 4 * DIM:5 * DIM],
                              start=True, stop=True).then_inc(pe_done.h, 1)
            vv_done.passed(1)
            pe_done.passed(1)
            node_linear([(T1, DIM, 0)], [dict(w=[wcol(0)], add=wcol(1), to=(T1, DIM, 0))], T2)
            with nc.Block() as block:
                @block.vector
                def _(dve):
                    c = vch.on(dve)
                    c.link(V.tensor_tensor(sums, sums, each(has[:, :], DIM), ALU.mult))
            node_linear([(H, DIM, 0), (T1, DIM, 0)],
                        [dict(w=[wcol(2), wcol(3)], add=wcol(5), relu=True, to=(T1, DIM, 0))], T2)
            node_linear([(T1, DIM, 0)], [dict(w=[wcol(6)], add=wcol(7), plus=(X, DIM, 0), to=(X, DIM, 0))], T2)

        def step_neighbours():
            rows = [T2[0:HEADS, k * ALL:(k + 1) * ALL] for k in range(4)]
            with nc.Block() as block:
                @block.sync
                def _(sp):
                    with nc.allow_non_contiguous_dma(reason="one edge of each step"):
                        for row, (s0, e) in zip(rows, ((1, P - 1), (0, P - 1), (1, 0), (2, 0))):
                            src = step_dst_d[s0:s0 + ALL, e:e + 1].rearrange("s e -> e s").to_broadcast([HEADS, ALL])
                            sp.dma_start(row, src).then_inc(loaded.h, 16)
                    sp.wait_ge(loaded.h, loaded.at(64))

                @block.vector
                def _(dve):
                    c = vch.on(dve)
                    dve.wait_ge(loaded.h, loaded.at(64))
                    for k, to in enumerate((goes_on, came_on)):
                        c.link(V.tensor_tensor(to[:, :], rows[2 * k], rows[2 * k + 1], ALU.not_equal))
                        c.link(V.tensor_scalar(to[:, :], to[:, :], -BIG, None, ALU.mult))
            loaded.passed(64)

        def edge_logits(heads, width, table, att, we):
            *R8, M8 = (T1[:, k * TURN * WIDE:k * TURN * WIDE + TURN * width] for k in range(3))
            OT8 = T1[:, 6 * TURN * P:7 * TURN * P]
            per_bank = 512 // width
            spot = lambda g, u: PS[:, 2048 * g + u // per_bank * 512 + u % per_bank * width:][:, 0:width]
            W4 = GROUP * width
            kept = edge_rows_d[:, 0:STEPS * width]
            here, kept_here = (rows_here, odd_rows_here), (saved, odd_saved)
            with nc.Block() as block:
                @block.gpsimd
                def _(gp):
                    c = gch.on(gp)
                    with gp.Fori(0, (TURNS + 1) // 2) as j:
                        c.open(j, 4)
                        for odd in range(2):
                            turn = j * 2 + odd
                            for g in range(2):
                                gp.wait_ge(pA[g].h, pA[g].before(turn))
                                gp.sem_inc(pool_gate.h, 1)
                                gp.wait_ge(aA[g].h, aA[g].before(turn))
                                idx = slot_idx[:, 4 * g:4 * g + 4] if not odd else slot_idx2[:, 4 * g:4 * g + 4]
                                c.link(G.tensor_copy(idx, srci[:, bass.ds(turn * TURN + 4 * g, 4)]))
                                gp.sem_inc(pool_gate.h, 1)
                                for u in range(4):
                                    gp.indirect_dma_start(part(quad(R8[odd], g, width), u, width), None, table[:, :],
                                                          bass.IndirectOffsetOnAxis(ap=idx[:, u:u + 1], axis=0)).then_inc(here[odd][g].h, 16)
                    c.close((TURNS + 1) // 2)

                @block.sync
                def _(sp):
                    with sp.Fori(0, TURNS + 1) as j:
                        for g in range(2):
                            sp.wait_ge(pA[g].h, pA[g].last(j))
                            sp.dma_start(quad(OT8, g), onehot_t_d[:, bass.ds(j * TURN * P + g * GROUP * P, GROUP * P)]).then_inc(tiles_here[g].h, 16)

                @block.scalar
                def _(act):
                    for g in range(2):
                        aA[g].start(act)
                    with act.Fori(0, (TURNS + 1) // 2) as j:
                        for odd in range(2):
                            for g in range(2):
                                act.wait_ge(here[odd][g].h, here[odd][g].at(64 * j + 64))
                                act.dma_start(kept[:, bass.ds((j * 2 + odd) * (TURN * width) + g * W4, W4)],
                                              quad(R8[odd], g, width)).then_inc(kept_here[odd][g].h, 16)
                            for g in range(2):
                                act.wait_ge(kept_here[odd][g].h, kept_here[odd][g].at(16 * j + 16))
                                act.sem_inc(aA[g].h, 1)

                @block.tensor
                def _(pe):
                    for g in range(2):
                        pA[g].start(pe)
                    with pe.Fori(0, (TURNS + 1) // 2) as j:
                        for odd in range(2):
                            turn = j * 2 + odd
                            bs = blocks_of(pe, turn)
                            for g in range(2):
                                pe.wait_ge(tiles_here[g].h, tiles_here[g].at(32 * j + (16 * odd + 16)))
                                pe.wait_ge(here[odd][g].h, here[odd][g].at(64 * j + 64))
                                pe.wait_ge(vA[g].h, vA[g].last(turn))
                                for u in range(4):
                                    T_.matmul(spot(g, u), part(quad(OT8, g), u), T2[:, bass.ds(bs[4 * g + u] * width, width)], start=True, stop=False)
                                    last = T_.matmul(spot(g, u), ident[:, :], part(quad(R8[odd], g, width), u, width), start=False, stop=True)
                                last.then_inc(pA[g].h, 1)

                @block.vector
                def _(dve):
                    c = vch.on(dve)
                    c.link(V.memset(LG[:, :], 0.0))
                    for g in range(2):
                        vA[g].start(dve)
                    with dve.Fori(0, TURNS + 1) as j:
                        c.open(j, 4)
                        s0 = j * TURN
                        ms = [quad(M8, g, width) for g in range(2)]
                        for g in range(2):
                            dve.wait_ge(pA[g].h, pA[g].turn(j))
                            for u in range(4):
                                last = V.scalar_tensor_tensor(part(ms[g], u, width), we, ew[:, bass.ds(s0 + 4 * g + u, 1)], spot(g, u), ALU.mult, ALU.add)
                            last.then_inc(vA[g].h, 1)
                            dve.wait_ge(vA[g].h, vA[g].turn(j))
                            c.link(V.scalar_tensor_tensor(ms[g], ms[g], 0.2, ms[g], ALU.mult, ALU.max))
                            c.link(V.tensor_tensor(split(ms[g], width), split(ms[g], width), every(att, 4), ALU.mult))
                            V.tensor_reduce(LG[:, bass.ds((s0 + 4 * g) * heads, 4 * heads)], split(ms[g], width // heads), AX.X, ALU.add)
                    c.close(TURNS + 1)
            for g in range(2):
                for s in (pA, aA, vA):
                    s[g].passed(TURNS + 2)
                for odd in range(2):
                    here[odd][g].passed(32 * (TURNS + 1))
                    kept_here[odd][g].passed(8 * (TURNS + 1))
                tiles_here[g].passed(16 * (TURNS + 1))
            pool_gate.passed(4 * (TURNS + 1))

        def segment_weights(heads):
            n = CHUNKS * heads * P
            L, F, B = (T1[:, k * 3584:k * 3584 + n] for k in range(3))
            mask = T2[:, 0:n]
            dst_r, mf, mb, eq, tmp, valid = (T2[:, 3584 + k * ALL:3584 + (k + 1) * ALL] for k in range(6))
            rowF, rowB = (T2[0:heads, 3584 + (6 + k) * ALL:3584 + (7 + k) * ALL] for k in range(2))
            k0 = 3584 + 8 * ALL
            prev, nxt = T2[:, k0:k0 + CHUNKS], T2[:, k0 + 8:k0 + 8 + CHUNKS]
            eF, eB, cF, cB = (T2[:, k0 + 16 + 32 * k:k0 + 16 + 32 * k + CHUNKS * heads] for k in range(4))
            nobody = T2[0:heads, k0 + 144:k0 + 145]
            che = lambda ap: ap.rearrange("p (c h e) -> p c h e", h=heads, e=P)
            ce = lambda ap: ap.rearrange("p (c e) -> p c e", e=P)
            ch = lambda ap: ap.rearrange("p (c h) -> p c h", h=heads)
            lgs = LG[:, 0:ALL * heads].rearrange("p (s h) -> p s h", h=heads)
            rows_of = lambda d: d.rearrange("(c p) e -> p c e", p=P)
            ends = lambda d, o: d[0:heads, o:o + ALL].rearrange("h (c p) -> p h c", p=P)
            with nc.Block() as block:
                @block.sync
                def _(sp):
                    sp.dma_start(ce(dst_r), rows_of(step_dst_d[1:ALL + 1, :])).then_inc(loaded.h, 16)
                    sp.dma_start(ce(mf), rows_of(step_first_d)).then_inc(loaded.h, 16)
                    sp.dma_start(ce(mb), rows_of(step_last_d)).then_inc(loaded.h, 16)
                    with nc.allow_non_contiguous_dma(reason="one number of each step"):
                        sp.dma_start(prev.unsqueeze(2), rows_of(step_dst_d[0:ALL, P - 1:P])).then_inc(loaded.h, 16)
                        sp.dma_start(nxt.unsqueeze(2), rows_of(step_dst_d[2:ALL + 2, 0:1])).then_inc(loaded.h, 16)
                        sp.wait_ge(vv_done.h, vv_done.at(2))
                        for h in range(heads):
                            for d, e in ((ends_d, eF), (ends2_d, eB)):
                                sp.dma_start(d[h:h + 1, 1:ALL + 1].rearrange("a (c p) -> p c a", p=P), ch(e)[:, :, h:h + 1]).then_inc(stored.h, 16)
                        sp.wait_ge(stored.h, stored.at(32 * heads))
                        sp.dma_start(rowF, ends_d[0:heads, 1:ALL + 1]).then_inc(loaded.h, 16)
                        sp.dma_start(rowB, ends2_d[0:heads, 1:ALL + 1]).then_inc(loaded.h, 16)
                        sp.wait_ge(vv_done.h, vv_done.at(3))
                        for d, row in ((ends_d, rowF), (ends2_d, rowB)):
                            sp.dma_start(d[0:heads, 1:ALL + 1], row).then_inc(stored.h, 16)
                            sp.dma_start(d[0:heads, 0:1], nobody).then_inc(stored.h, 16)
                            sp.dma_start(d[0:heads, ALL + 1:ALL + 2], nobody).then_inc(stored.h, 16)
                        sp.wait_ge(stored.h, stored.at(32 * heads + 96))
                        for h in range(heads):
                            for d, o, cc in ((ends_d, 0, cF), (ends2_d, 2, cB)):
                                sp.dma_start(ch(cc)[:, :, h:h + 1], d[h:h + 1, o:o + ALL].rearrange("a (c p) -> p c a", p=P)).then_inc(loaded.h, 16)
                    sp.wait_ge(loaded.h, loaded.at(16 * 7 + 32 * heads))

                @block.vector
                def _(dve):
                    c = vch.on(dve)
                    c.link(V.tensor_scalar(valid, dloc[:, :], 0.0, None, ALU.is_ge))
                    c.link(V.scalar_tensor_tensor(valid, dloc[:, :], float(P), valid, ALU.is_lt, ALU.mult))
                    V.memset(nobody, -BIG)
                    c.link(V.tensor_scalar(tmp, valid, BIG, -BIG, ALU.mult, ALU.add))
                    c.link(V.tensor_tensor(lgs, lgs, each(valid, heads), ALU.mult))
                    V.tensor_tensor(lgs, lgs, each(tmp, heads), ALU.add).then_inc(vv_done.h, 1)
                    dve.wait_ge(loaded.h, loaded.at(80))
                    dve.wait_ge(ac_done.h, ac_done.at(1))
                    for src, edge, to, way in ((mf, 0, F, 1), (mb, P - 1, B, -1)):
                        for h in range(heads):
                            c.link(V.tensor_copy(che(mask)[:, :, h], ce(src)))
                        c.link(V.memset(che(mask)[:, :, :, edge], -BIG))
                        c.link(V.tensor_tensor_scan(to[:, ::way], mask[:, ::way], L[:, ::way], -BIG, ALU.add, ALU.max))
                    c.link(V.tensor_tensor(F, F, B, ALU.max))
                    c.link(V.tensor_copy(ch(eF), che(F)[:, :, :, P - 1]))
                    V.tensor_copy(ch(eB), che(F)[:, :, :, 0]).then_inc(vv_done.h, 1)
                    dve.wait_ge(loaded.h, loaded.at(112))
                    c.link(V.tensor_tensor_scan(T1[0:heads, 7168:7168 + ALL], goes_on[0:heads, :], rowF, -BIG, ALU.add, ALU.max))
                    c.link(V.tensor_tensor_scan(T1[0:heads, 7168 + ALL:7168 + 2 * ALL][:, ::-1], came_on[0:heads, ::-1], rowB[:, ::-1], -BIG, ALU.add, ALU.max))
                    c.link(V.tensor_copy(rowF, T1[0:heads, 7168:7168 + ALL]))
                    V.tensor_copy(rowB, T1[0:heads, 7168 + ALL:7168 + 2 * ALL]).then_inc(vv_done.h, 1)
                    dve.wait_ge(loaded.h, loaded.at(16 * 7 + 32 * heads))
                    for border, carry in ((prev, cF), (nxt, cB)):
                        c.link(V.tensor_tensor(ce(eq), ce(dst_r), each(border, P), ALU.is_equal))
                        c.link(V.tensor_scalar(eq, eq, BIG, -BIG, ALU.mult, ALU.add))
                        for h in range(heads):
                            c.link(V.tensor_tensor(ce(tmp), ce(eq), each(ch(carry)[:, :, h], P), ALU.add))
                            c.link(V.tensor_tensor(che(F)[:, :, h], che(F)[:, :, h], ce(tmp), ALU.max))
                    dve.sem_inc(vv_done.h, 1)
                    dve.wait_ge(pe_done.h, pe_done.at(2))
                    back = PS[:, 0:n].rearrange("p (c h s) -> p c h s", h=heads, s=P)
                    lgc = LG[:, 0:ALL * heads].rearrange("p (c s h) -> p c s h", s=P, h=heads)
                    for h in range(heads):
                        last = V.tensor_tensor(lgc[:, :, :, h], lgc[:, :, :, h], back[:, :, h], ALU.subtract)
                    last.then_inc(vv_done.h, 1)
                    dve.wait_ge(ac_done.h, ac_done.at(2))
                    c.link(V.tensor_tensor(lgs, lgs, each(valid, heads), ALU.mult))

                @block.tensor
                def _(pe):
                    pe.wait_ge(vv_done.h, vv_done.at(1))
                    for k in range(CHUNKS):
                        for h in range(heads):
                            o = (k * heads + h) * P
                            last = T_.transpose(PS[:, o:o + P], lgs[:, k * P:(k + 1) * P, h], ident[:, :])
                    last.then_inc(pe_done.h, 1)
                    pe.wait_ge(vv_done.h, vv_done.at(4))
                    for k in range(CHUNKS * heads):
                        last = T_.transpose(PS[:, k * P:(k + 1) * P], F[:, k * P:(k + 1) * P], ident[:, :])
                    last.then_inc(pe_done.h, 1)

                @block.scalar
                def _(act):
                    act.wait_ge(pe_done.h, pe_done.at(1))
                    S_.activation(L, PS[:, 0:n], ACT.Copy).then_inc(ac_done.h, 1)
                    act.wait_ge(vv_done.h, vv_done.at(5))
                    S_.activation(LG[:, 0:ALL * heads], LG[:, 0:ALL * heads], ACT.Exp).then_inc(ac_done.h, 1)
            for s, k in ((loaded, 112 + 32 * heads), (stored, 32 * heads + 96), (vv_done, 5), (pe_done, 2), (ac_done, 2)):
                s.passed(k)

        def weighted_sums(heads, width):
            both = width + heads
            one = heads == 1
            R8 = T2[:, 0:TURN * width]
            M8 = T2[:, TURN * WIDE:TURN * WIDE + TURN * both]
            O8 = T2[:, 5 * TURN * P:6 * TURN * P]
            tables = [T1[:, k * BLOCKS * both:(k + 1) * BLOCKS * both] for k in range(1 + one)]
            rows_used = aA if one else vA
            W4 = GROUP * width
            kept = edge_rows_d[:, 0:STEPS * width]
            with nc.Block() as block:
                @block.sync
                def _(sp):
                    with sp.Fori(0, TURNS) as j:
                        for g in range(2):
                            sp.wait_ge(rows_used[g].h, rows_used[g].last(j))
                            sp.dma_start(quad(R8, g, width), kept[:, bass.ds((j + 1) * (TURN * width) + g * W4, W4)]).then_inc(tiles_here[g].h, 16)

                @block.tensor
                def _(pe):
                    for g in range(2):
                        pA[g].start(pe)
                    pe.wait_ge(vv_done.h, vv_done.at(1))
                    with pe.Fori(0, TURNS) as j:
                        for g in range(2):
                            pe.wait_ge(vA[g].h, vA[g].last(j))
                            pe.wait_ge(aA[g].h, aA[g].last(j))
                            pe.wait_ge(vB[g].h, vB[g].last(j))
                            for u in range(4):
                                last = T_.matmul(bank(4 * g + u, both), part(quad(O8, g), u), part(quad(M8, g, both), u, both), start=True, stop=True)
                            last.then_inc(pA[g].h, 1)

                @block.scalar
                def _(act):
                    for g in range(2):
                        aA[g].start(act)
                    with act.Fori(0, TURNS) as j:
                        for g in range(2):
                            s1 = (j + 1) * TURN + 4 * g
                            act.wait_ge(pA[g].h, pA[g].turn(j))
                            if one:
                                act.wait_ge(tiles_here[g].h, tiles_here[g].at(16 * j + 16))
                            act.sem_inc(scalar_gate.h, 1)
                            M4 = quad(M8, g, both)
                            copy = S_.activation(split(M4, both)[:, :, width:both],
                                                 split(LG[:, bass.ds(s1 * heads, 4 * heads)], heads), ACT.Copy)
                            if one:
                                for u in range(4):
                                    copy = S_.activation(M4[:, u * both:u * both + width], part(quad(R8, g, width), u, width),
                                                         ACT.Copy, scale=LG[:, bass.ds(s1 + u, 1)])
                            copy.then_inc(aA[g].h, 1)

                @block.vector
                def _(dve):
                    c = vch.on(dve)
                    V.memset(O8, 0.0)
                    V.memset(M8, 0.0).then_inc(vv_done.h, 1)
                    c.link(V.memset(T1[:, 0:len(tables) * BLOCKS * both], 0.0))
                    for g in range(2):
                        vA[g].start(dve)
                        vB[g].start(dve)
                    w = width // heads
                    with dve.Fori(0, TURNS) as j:
                        c.open(j, 8)
                        bs = blocks_of(dve, j)
                        for g in range(2):
                            s1 = (j + 1) * TURN + 4 * g
                            dve.wait_ge(pA[g].h, pA[g].turn(j))
                            hots = one_hot(O8, g, dloc, s1)
                            if one:
                                hots.then_inc(vA[g].h, 1)
                                add_to_table(c, tables, both, bs[4 * g:4 * g + 4], [bank(4 * g + u, both) for u in range(4)])
                            else:
                                dve.wait_ge(tiles_here[g].h, tiles_here[g].at(16 * j + 16))
                                for u in range(4):
                                    o = T1[:, bass.ds(bs[4 * g + u] * both, both)]
                                    V.tensor_tensor(o, o, bank(4 * g + u, both), ALU.add).then_inc(vch.s.h, 1)
                                    last = V.tensor_tensor(split(quad(M8, g, both)[:, u * both:u * both + width], w), split(part(quad(R8, g, width), u, width), w),
                                                           each(LG[:, bass.ds((s1 + u) * heads, heads)], w), ALU.mult)
                                    c.k += 1
                                    if u == 3:
                                        last.then_inc(vA[g].h, 1)
                                    dve.wait_ge(vch.s.h, j * 8 + vch.s.at(c.k))
                            dve.sem_inc(vB[g].h, 1)
                    c.close(TURNS)
                    if one:
                        c.link(V.tensor_tensor(tables[0], tables[0], tables[1], ALU.add))
            vv_done.passed(1)
            scalar_gate.passed(2 * TURNS)
            for g in range(2):
                for s in (pA, aA, vA, vB):
                    s[g].passed(TURNS + 1)
                tiles_here[g].passed(16 * TURNS)

        def norm_prelu(heads, width, col):
            both = width + heads
            y, z = blocks(T2, width), blocks(T1, width)
            num = blocks(T1, both)
            rden = LG[:, 0:BLOCKS * heads].rearrange("p (t h) -> p t h", h=heads)
            cb, gamma, beta = (W[:, col + k * width:col + (k + 1) * width] for k in range(3))
            tot = LG[:, 1024:1024 + width]
            scale = LG[:, 1536:1536 + width]
            real = small[:, 50:51]
            left = NODES - (BLOCKS - 1) * P
            pa = pa_col[:, 0:1]

            def totals(dve, c, tab, ready, passed):
                c.link(V.tensor_reduce(scale, tab.rearrange("p t f -> p f t"), AX.X, ALU.add))
                dve.sem_inc(vv_done.h, 1)
                dve.wait_ge(pe_done.h, pe_done.at(ready))
                c.link(V.tensor_scalar(tot, bank(0, width), 1.0 / NODES, None, ALU.mult))

            with nc.Block() as block:
                @block.vector
                def _(dve):
                    c = vch.on(dve)
                    c.link(V.tensor_scalar(real, pcol[:, :], float(left), None, ALU.is_lt))
                    c.link(V.tensor_scalar(rden, num[:, :, width:both], 1e-16, None, ALU.add))
                    c.link(V.reciprocal(LG[:, 0:BLOCKS * heads], LG[:, 0:BLOCKS * heads]))
                    w = width // heads
                    for h in range(heads):
                        c.link(V.tensor_tensor(y[:, :, h * w:(h + 1) * w], num[:, :, h * w:(h + 1) * w], each(rden[:, :, h], w), ALU.mult))
                    c.link(V.tensor_tensor(y, y, every(cb, BLOCKS), ALU.add))
                    c.link(V.tensor_scalar(y[:, BLOCKS - 1], y[:, BLOCKS - 1], real, None, ALU.mult))
                    totals(dve, c, y, 1, 1)
                    c.link(V.tensor_tensor(y, y, every(tot, BLOCKS), ALU.subtract))
                    c.link(V.tensor_scalar(y[:, BLOCKS - 1], y[:, BLOCKS - 1], real, None, ALU.mult))
                    c.link(V.tensor_tensor(z, y, y, ALU.mult))
                    totals(dve, c, z, 2, 2)
                    V.tensor_scalar(tot, tot, 1e-5, None, ALU.add).then_inc(vv_done.h, 1)
                    dve.wait_ge(ac_done.h, ac_done.at(1))
                    c.link(V.reciprocal(scale, tot))
                    c.link(V.tensor_tensor(scale, scale, gamma, ALU.mult))
                    c.link(V.tensor_tensor(y, y, every(scale, BLOCKS), ALU.mult))
                    c.link(V.tensor_tensor(y, y, every(beta, BLOCKS), ALU.add))
                    c.link(V.tensor_scalar(z, y, 0.0, pa, ALU.min, ALU.mult))
                    c.link(V.scalar_tensor_tensor(y, y, 0.0, z, ALU.max, ALU.add))

                @block.tensor
                def _(pe):
                    for k in range(2):
                        pe.wait_ge(vv_done.h, vv_done.at(k + 1))
                        T_.matmul(bank(0, width), ones[:, :], scale, start=True, stop=True).then_inc(pe_done.h, 1)

                @block.scalar
                def _(act):
                    act.wait_ge(vv_done.h, vv_done.at(3))
                    S_.activation(tot, tot, ACT.Sqrt).then_inc(ac_done.h, 1)
            vv_done.passed(3)
            pe_done.passed(2)
            ac_done.passed(1)

        def layer2():
            step_neighbours()
            layernorm()
            row = lambda name, c0=0: I[name][c0:c0 + DIM]
            halves = lambda name, at: [(at + k * DIM, P, I[name][:, k * DIM:(k + 1) * DIM]) for k in range(2)]
            load_weights(halves("L2_Wl1", 0) + halves("L2_Wr1", 2 * DIM) + [
                (4 * DIM, P, bias_row(I["L2_bl1"], WIDE)), (6 * DIM, P, bias_row(I["L2_br1"], WIDE))])
            node_linear([(H, DIM, 0)], [dict(w=[wcol(k)], add=wcol(4 + k), to=(T1, WIDE, k * DIM)) for k in range(2)], T2)
            table_to_dram(T1, WIDE, wide_d)
            node_linear([(H, DIM, 0)], [dict(w=[wcol(2 + k)], add=wcol(6 + k), to=(T2, WIDE, k * DIM)) for k in range(2)], T1)
            flat = lambda ap: ap.rearrange("h c -> (h c)")
            load_weights([(0, P, bias_row(flat(I["L2_att1"]), WIDE)), (2 * DIM, P, bias_row(flat(I["L2_We1"]), WIDE))])
            edge_logits(HEADS, WIDE, wide_d, W[:, 0:WIDE], W[:, WIDE:2 * WIDE])
            segment_weights(HEADS)
            weighted_sums(HEADS, WIDE)
            load_weights([(k * WIDE, P, bias_row(I[n], WIDE)) for k, n in enumerate(("L2_cb1", "L2_bng1", "L2_bnb1"))])
            with nc.Block() as block:
                @block.sync
                def _(sp):
                    sp.dma_start(pa_col[:, :], bias_row(I["L2_pa"], 1)).then_inc(loaded.h, 16)
                    sp.wait_ge(loaded.h, loaded.at(16))
            loaded.passed(16)
            norm_prelu(HEADS, WIDE, 0)
            load_weights([((2 * k + i) * DIM, P, I[n][i * P:(i + 1) * P, :]) for k, n in enumerate(("L2_Wl2", "L2_Wr2")) for i in range(2)]
                         + [(4 * DIM, P, bias_row(I["L2_bl2"])), (5 * DIM, P, bias_row(I["L2_br2"]))])
            node_linear([(T2, WIDE, 0), (T2, WIDE, DIM)],
                        [dict(w=[wcol(0), wcol(1)], add=wcol(4), to=(T1, DIM, 0)),
                         dict(w=[wcol(2), wcol(3)], add=wcol(5), to=(T1[:, ROWS:2 * ROWS], DIM, 0))], LG)
            table_to_dram(T1, DIM, gather_d)
            with nc.Block() as block:
                @block.scalar
                def _(act):
                    S_.activation(T2[:, 0:ROWS], T1[:, ROWS:2 * ROWS], ACT.Copy)
            load_weights([(0, P, bias_row(flat(I["L2_att2"]))), (DIM, P, bias_row(flat(I["L2_We2"])))])
            edge_logits(1, DIM, gather_d, wcol(0), wcol(1))
            segment_weights(1)
            weighted_sums(1, DIM)
            load_weights([(k * DIM, P, bias_row(I[n])) for k, n in enumerate(("L2_cb2", "L2_bng2", "L2_bnb2"))])
            norm_prelu(1, DIM, 0)
            load_weights([(0, P, I["L2_skipW"]), (DIM, P, bias_row(I["L2_skipb"]))])
            node_linear([(H, DIM, 0)], [dict(w=[wcol(0)], add=wcol(1), plus=(X, DIM, 0), to=(X, DIM, 0))], T1)
            with nc.Block() as block:
                @block.vector
                def _(dve):
                    c = vch.on(dve)
                    c.link(V.tensor_tensor(X[:, :], X[:, :], T2[:, 0:ROWS], ALU.add))

        def edge_maxima():
            R8, M8, RT8, SC8, ST8, O8, OT8, MK8 = (T2[:, k * TURN * P:(k + 1) * TURN * P] for k in range(8))
            w2 = wcol(2)
            maxima = T1[:, ROWS:2 * ROWS]
            with nc.Block() as block:
                @block.gpsimd
                def _(gp):
                    gather_rows(gp, gather_d, R8, DIM, lambda g, j: gp.wait_ge(vA[g].h, vA[g].last(j)), ahead=1)

                @block.sync
                def _(sp):
                    with sp.Fori(0, TURNS) as j:
                        for g in range(2):
                            sp.wait_ge(vB[g].h, vB[g].last(j))
                            row = step_first_d[bass.ds(j * TURN + 4 * g, 4), :].rearrange("(a s) e -> a (s e)", a=1)
                            sp.dma_start(quad(MK8, g), row.to_broadcast([P, GROUP * P])).then_inc(extra_here[g].h, 16)
                            sp.wait_ge(pA[g].h, pA[g].last(j))
                            sp.dma_start(quad(OT8, g), onehot_t_d[:, bass.ds((j + 1) * (TURN * P) + g * GROUP * P, GROUP * P)]).then_inc(tiles_here[g].h, 16)

                @block.tensor
                def _(pe):
                    for g in range(2):
                        for s in (pA, pB, pC, pD, pE):
                            s[g].start(pe)
                    with pe.Fori(0, TURNS) as j:
                        bs = blocks_of(pe, j + 1)
                        for g in range(2):
                            pe.wait_ge(tiles_here[g].h, tiles_here[g].at(16 * j + 16))
                            pe.wait_ge(vA[g].h, vA[g].last(j))
                            for u in range(4):
                                last = T_.matmul(part(bank(g), u), part(quad(OT8, g), u), T1[:, bass.ds(bs[4 * g + u] * DIM, DIM)], start=True, stop=True)
                            last.then_inc(pA[g].h, 1)
                        for g in range(2):
                            pe.wait_ge(vB[g].h, vB[g].turn(j))
                            pe.wait_ge(vD[g].h, vD[g].last(j))
                            for u in range(4):
                                last = T_.transpose(part(bank(6 + g), u), part(quad(SC8, g), u), ident[:, :])
                            last.then_inc(pD[g].h, 1)

                        def rows_down(g):
                            pe.wait_ge(vA[g].h, vA[g].turn(j))
                            pe.wait_ge(aA[g].h, aA[g].last(j))
                            for u in range(4):
                                last = T_.transpose(part(bank(2 + g), u), part(quad(M8, g), u), ident[:, :])
                            last.then_inc(pB[g].h, 1)

                        def last_edges(g):
                            pe.wait_ge(aB[g].h, aB[g].turn(j))
                            pe.wait_ge(vC[g].h, vC[g].turn(j))
                            for u in range(4):
                                last = T_.matmul(part(bank(6 + g), u), part(quad(O8, g), u), part(quad(ST8, g), u), start=True, stop=True)
                            last.then_inc(pE[g].h, 1)

                        def times_w2(g):
                            pe.wait_ge(aA[g].h, aA[g].turn(j))
                            pe.wait_ge(vB[g].h, vB[g].turn(j))
                            T_.matmul(bank(4 + g), w2, quad(RT8, g), start=True, stop=True).then_inc(pC[g].h, 1)

                        rows_down(0)
                        last_edges(0)
                        last_edges(1)
                        rows_down(1)
                        times_w2(0)
                        times_w2(1)

                @block.scalar
                def _(act):
                    for g in range(2):
                        aA[g].start(act)
                        aB[g].start(act)
                    with act.Fori(0, TURNS) as j:
                        for g in range(2):
                            act.wait_ge(pD[g].h, pD[g].turn(j))
                            act.wait_ge(pE[g].h, pE[g].last(j))
                            S_.activation(quad(ST8, g), bank(6 + g), ACT.Copy).then_inc(aB[g].h, 1)
                        for g in range(2):
                            act.wait_ge(pB[g].h, pB[g].turn(j))
                            act.wait_ge(pC[g].h, pC[g].last(j))
                            S_.activation(quad(RT8, g), bank(2 + g), ACT.Relu).then_inc(aA[g].h, 1)

                @block.vector
                def _(dve):
                    c = vch.on(dve)
                    V.memset(SC8, -BIG)
                    V.memset(PS[:, 4 * 512:6 * 512], 0.0)
                    V.memset(maxima, 0.0)
                    c.link(V.memset(H[:, :], 0.0))
                    for g in range(2):
                        for s in (vA, vB, vC, vD):
                            s[g].start(dve)
                    with dve.Fori(0, TURNS) as j:
                        c.open(j, 8)
                        bs = blocks_of(dve, j)

                        def scan(g):
                            dve.wait_ge(extra_here[g].h, extra_here[g].at(16 * j + 16))
                            dve.wait_ge(pC[g].h, pC[g].last(j))
                            dve.wait_ge(pD[g].h, pD[g].last(j))
                            before = 1 - g
                            dve.wait_ge(vB[before].h, vB[before].turn(j) if g else vB[before].last(j))
                            V.tensor_tensor_scan(quad(SC8, g), quad(MK8, g), bank(4 + g), quad(SC8, before)[:, GROUP * P - 1:GROUP * P],
                                                 ALU.add, ALU.max).then_inc(vB[g].h, 1)

                        def add_rows(g):
                            dve.wait_ge(rows_here[g].h, rows_here[g].at(64 * j + 64))
                            dve.wait_ge(pA[g].h, pA[g].turn(j))
                            dve.wait_ge(pB[g].h, pB[g].last(j))
                            V.tensor_tensor(quad(M8, g), bank(g), quad(R8, g), ALU.add).then_inc(vA[g].h, 1)

                        def last_edge_hots(g):
                            dve.wait_ge(pE[g].h, pE[g].last(j))
                            one_hot(O8, g, dend, j * TURN + 4 * g).then_inc(vC[g].h, 1)

                        scan(0)
                        scan(1)
                        add_rows(0)
                        last_edge_hots(0)
                        last_edge_hots(1)
                        for g in range(2):
                            if g == 1:
                                add_rows(1)
                            dve.wait_ge(pE[g].h, pE[g].turn(j))
                            add_to_table(c, (maxima, H), DIM, bs[4 * g:4 * g + 4], [part(bank(6 + g), u) for u in range(4)])
                            dve.sem_inc(vD[g].h, 1)
                    c.close(TURNS)
            for g in range(2):
                for s in (pA, pB, pC, pD, pE, aA, aB, vA, vB, vC, vD):
                    s[g].passed(TURNS + 1)
                rows_here[g].passed(64 * TURNS)
                tiles_here[g].passed(16 * TURNS)
                extra_here[g].passed(16 * TURNS)
            pool_gate.passed(2 * TURNS)

        def layer3():
            layernorm()
            for n, name in enumerate(("in", "hid", "out")):
                w1 = I[f"L3_W1_{name}"]
                load_weights([(0, P, w1[0:DIM, :]), (DIM, P, w1[DIM:2 * DIM, :]), (2 * DIM, P, I[f"L3_W2_{name}"]),
                              (3 * DIM, P, bias_row(I[f"L3_b1_{name}"])), (4 * DIM, P, bias_row(I[f"L3_b2_{name}"]))])
                with nc.Block() as block:
                    @block.vector
                    def _(dve):
                        c = vch.on(dve)
                        c.link(V.tensor_tensor(wcol(0), wcol(0), wcol(1), ALU.subtract))
                        c.link(V.memset(wcol(5), 0.0))
                node_linear([(H, DIM, 0)], [dict(w=[wcol(0)], add=wcol(3), to=(T1, DIM, 0)),
                                            dict(w=[wcol(1)], add=wcol(5), to=(T1[:, ROWS:2 * ROWS], DIM, 0))], T2)
                table_to_dram(T1[:, ROWS:2 * ROWS], DIM, gather_d)
                edge_maxima()
                m, h = blocks(T1[:, ROWS:2 * ROWS], DIM), blocks(H, DIM)
                with nc.Block() as block:
                    @block.vector
                    def _(dve):
                        c = vch.on(dve)
                        c.link(V.tensor_tensor(m, m, h, ALU.add))
                        c.link(V.tensor_tensor(m, m, every(wcol(4), BLOCKS), ALU.add))
                        c.link(V.tensor_tensor(m, m, each(has[:, :], DIM), ALU.mult))
                        if n < 2:
                            c.link(V.tensor_scalar(h, m, 0.0, None, ALU.max))
                        else:
                            c.link(V.tensor_tensor(X[:, :], X[:, :], T1[:, ROWS:2 * ROWS], ALU.add))

        def give_back():
            with nc.Block() as block:
                @block.sync
                def _(sp):
                    full = NODES // P
                    sp.dma_start(out[0:full * P, :].rearrange("(t p) f -> p t f", p=P), blocks(X, DIM)[:, 0:full]).then_inc(stored.h, 16)
                    sp.dma_start(out[full * P:NODES, :], X[0:NODES - full * P, full * DIM:BLOCKS * DIM]).then_inc(stored.h, 16)
                    sp.wait_ge(stored.h, stored.at(32))
            stored.passed(32)

        setup()
        layers = (layer0, layer1, layer2, layer3)
        for layer in layers:
            layer()
        give_back()


def kernel(**inputs):
    import concourse.bacc as bacc
    from concourse.bass_utils import run_bass_kernel_spmd as run

    a = {k: np.asarray(v) for k, v in inputs.items()}

    def filled(v, shape, fill, at=0):
        r = np.full(shape, fill, v.dtype)
        r[at:at + v.shape[0]] = v
        return r

    arrays = {
        "x": filled(a["x"], (ROWS, DIM), 0),
        "src": filled(a["src"], (ALL * P,), 0),
        "dst": filled(a["dst"], (ALL * P + 2,), 1 << 20, 1),
        "ew": filled(a["edge_weight1"].reshape(-1), (ALL * P,), 0),
        "ea": filled(a["edge_attr_64"], (TILES * P, EDGE_DIM), 0),
    }
    arrays["dst"][0] = -1
    for k, v in a.items():
        if k.startswith("L"):
            arrays[k.replace("_gnn_", "_")] = v.reshape(-1) if v.ndim == 0 or k == "L0_gnn_a_w" else v
    arrays["L0_a_w2"] = arrays["L0_a_w"][DIM:]
    arrays["L0_a_w"] = arrays["L0_a_w"][:DIM]
    arrays = {k: np.ascontiguousarray(v) for k, v in arrays.items()}
    nc = bacc.Bacc("TRN2", target_bir_lowering=False, num_devices=1)
    ins = {k: nc.dram_tensor(f"in_{k}", v.shape, mybir.dt.from_np(v.dtype), kind="ExternalInput").ap()
           for k, v in arrays.items()}
    out = nc.dram_tensor("out", (NODES, DIM), FP32, kind="ExternalOutput").ap()
    build(nc, ins, out)
    got = run(nc, [{f"in_{k}": v for k, v in arrays.items()}], core_ids=[0])
    return got.results[0]["out"]
```
